# Optimizing a Trainium2 kernel written in Bass

```python
import numpy as np
import jax
import jax.numpy as jnp

def _softmax(x, axis=-1):
    return jax.nn.softmax(x, axis=axis)

def _gelu(x):
    return jax.nn.gelu(x, approximate=True)

def _silu(x):
    return jax.nn.silu(x)

def _sigmoid(x):
    return jax.nn.sigmoid(x)

def _layernorm(x, axis=-1, eps=1e-05):
    m = jnp.mean(x, axis=axis, keepdims=True)
    v = jnp.var(x, axis=axis, keepdims=True)
    return (x - m) / jnp.sqrt(v + eps)

def _scatter_add(tgt, idx, src, axis=0):
    return tgt.at[idx].add(src)

def _segment_sum(src, seg, n):
    return jax.ops.segment_sum(src, seg, n)
kernel_name = 'mk_gnn_resnorm_d2_gnn_r8_c13434'

def setup_inputs(seed: int=0):
    np.random.seed(seed)
    _w = jnp.asarray

    def _rec_inputs():
        import jax
        import jax.numpy as jnp
        _gk = jax.random.key(seed)
        x = -7.329e-05 + 0.9999 * jax.random.normal(jax.random.fold_in(_gk, 1), (1250, 1024), jnp.float32)
        src = jax.random.randint(jax.random.fold_in(_gk, 2), (20000,), 0, 1250, jnp.int32)
        dst = jax.random.randint(jax.random.fold_in(_gk, 3), (20000,), 0, 1250, jnp.int32)
        _o = jnp.argsort(dst, stable=True)
        src = src[_o]
        dst = dst[_o]
        return (x, src, dst)
    x, src, dst = _rec_inputs()

    def _L0_gnn_setup():
        import jax, jax.numpy as jnp
        import numpy as np
        N = 6250
        E = 100000
        D_IN = 1024
        D_HID = 512
        D_B = 256
        N_LAYERS = 3
        LN_EPS = 1e-05

        def layernorm(x, g, b):
            m = jnp.mean(x, axis=-1, keepdims=True)
            v = jnp.mean((x - m) ** 2, axis=-1, keepdims=True)
            return (x - m) * jax.lax.rsqrt(v + LN_EPS) * g + b
        key = jax.random.key(seed)
        ks = jax.random.split(key, 16)
        s = 0.02
        inp = {'x': jax.random.normal(ks[0], (N, D_IN), dtype=jnp.float32), 'edge_index': jax.random.randint(ks[1], (2, E), 0, N, dtype=jnp.int32), 'ln_in_g': jnp.ones((D_IN,), jnp.float32), 'ln_in_b': jnp.zeros((D_IN,), jnp.float32), 'W1': jax.random.normal(ks[2], (D_IN, D_HID), jnp.float32) * s, 'b1': jnp.zeros((D_HID,), jnp.float32), 'W2': jax.random.normal(ks[3], (D_HID, D_B), jnp.float32) * s, 'b2': jnp.zeros((D_B,), jnp.float32), 'layer_Wa': jax.random.normal(ks[4], (N_LAYERS, D_B, D_B), jnp.float32) * s, 'layer_ba': jnp.zeros((N_LAYERS, D_B), jnp.float32), 'layer_Wb': jax.random.normal(ks[5], (N_LAYERS, D_B, D_B), jnp.float32) * s, 'layer_bb': jnp.zeros((N_LAYERS, D_B), jnp.float32), 'layer_ng': jnp.ones((N_LAYERS, D_B), jnp.float32), 'layer_nb': jnp.zeros((N_LAYERS, D_B), jnp.float32), 'Wd1': jax.random.normal(ks[6], (D_B, D_HID), jnp.float32) * s, 'bd1': jnp.zeros((D_HID,), jnp.float32), 'Wd2': jax.random.normal(ks[7], (D_HID, D_IN), jnp.float32) * s, 'bd2': jnp.zeros((D_IN,), jnp.float32), 'out_g': jnp.ones((D_IN,), jnp.float32), 'out_b': jnp.zeros((D_IN,), jnp.float32)}
        return inp
    _L0_gnn_all = _L0_gnn_setup()
    _L0_gnn_in = {k: v for k, v in _L0_gnn_all.items() if k in ('ln_in_g', 'ln_in_b', 'W1', 'b1', 'W2', 'b2', 'layer_Wa', 'layer_ba', 'layer_Wb', 'layer_bb', 'layer_ng', 'layer_nb', 'Wd1', 'bd1', 'Wd2', 'bd2', 'out_g', 'out_b')}
    del _L0_gnn_all

    def _L1_gnn_setup():
        import jax, jax.numpy as jnp
        import numpy as np
        N_NODES = 3125
        N_EDGES = 50000
        D = 1024

        def _sage_layer(h, edge_src, edge_dst, deg_inv, W_self, W_neigh, b):
            msg = h[edge_src]
            agg = jax.ops.segment_sum(msg, edge_dst, num_segments=h.shape[0])
            mean = agg * deg_inv[:, None]
            return h @ W_self + mean @ W_neigh + b
        key = jax.random.key(seed)
        ks = jax.random.split(key, 8)
        s = 1.0 / np.sqrt(D)
        return {'x': jax.random.normal(ks[0], (N_NODES, D), dtype=jnp.float32), 'edge_src': jax.random.randint(ks[1], (N_EDGES,), 0, N_NODES, dtype=jnp.int32), 'edge_dst': jax.random.randint(ks[2], (N_EDGES,), 0, N_NODES, dtype=jnp.int32), 'W_self0': jax.random.normal(ks[3], (D, D), dtype=jnp.float32) * s, 'W_neigh0': jax.random.normal(ks[4], (D, D), dtype=jnp.float32) * s, 'b0': jnp.zeros((D,), dtype=jnp.float32), 'W_self1': jax.random.normal(ks[5], (D, D), dtype=jnp.float32) * s, 'W_neigh1': jax.random.normal(ks[6], (D, D), dtype=jnp.float32) * s, 'b1': jnp.zeros((D,), dtype=jnp.float32)}
    _L1_gnn_all = _L1_gnn_setup()
    _L1_gnn_in = {k: v for k, v in _L1_gnn_all.items() if k in ('W_self0', 'W_neigh0', 'b0', 'W_self1', 'W_neigh1', 'b1')}
    del _L1_gnn_all
    return {'x': x, 'src': src, 'dst': dst, 'L0_gnn_ln_in_g': _L0_gnn_in['ln_in_g'], 'L0_gnn_ln_in_b': _L0_gnn_in['ln_in_b'], 'L0_gnn_W1': _L0_gnn_in['W1'], 'L0_gnn_b1': _L0_gnn_in['b1'], 'L0_gnn_W2': _L0_gnn_in['W2'], 'L0_gnn_b2': _L0_gnn_in['b2'], 'L0_gnn_layer_Wa': _L0_gnn_in['layer_Wa'], 'L0_gnn_layer_ba': _L0_gnn_in['layer_ba'], 'L0_gnn_layer_Wb': _L0_gnn_in['layer_Wb'], 'L0_gnn_layer_bb': _L0_gnn_in['layer_bb'], 'L0_gnn_layer_ng': _L0_gnn_in['layer_ng'], 'L0_gnn_layer_nb': _L0_gnn_in['layer_nb'], 'L0_gnn_Wd1': _L0_gnn_in['Wd1'], 'L0_gnn_bd1': _L0_gnn_in['bd1'], 'L0_gnn_Wd2': _L0_gnn_in['Wd2'], 'L0_gnn_bd2': _L0_gnn_in['bd2'], 'L0_gnn_out_g': _L0_gnn_in['out_g'], 'L0_gnn_out_b': _L0_gnn_in['out_b'], 'L1_gnn_W_self0': _L1_gnn_in['W_self0'], 'L1_gnn_W_neigh0': _L1_gnn_in['W_neigh0'], 'L1_gnn_b0': _L1_gnn_in['b0'], 'L1_gnn_W_self1': _L1_gnn_in['W_self1'], 'L1_gnn_W_neigh1': _L1_gnn_in['W_neigh1'], 'L1_gnn_b1': _L1_gnn_in['b1']}

def reference(x, src, dst, L0_gnn_ln_in_g, L0_gnn_ln_in_b, L0_gnn_W1, L0_gnn_b1, L0_gnn_W2, L0_gnn_b2, L0_gnn_layer_Wa, L0_gnn_layer_ba, L0_gnn_layer_Wb, L0_gnn_layer_bb, L0_gnn_layer_ng, L0_gnn_layer_nb, L0_gnn_Wd1, L0_gnn_bd1, L0_gnn_Wd2, L0_gnn_bd2, L0_gnn_out_g, L0_gnn_out_b, L1_gnn_W_self0, L1_gnn_W_neigh0, L1_gnn_b0, L1_gnn_W_self1, L1_gnn_W_neigh1, L1_gnn_b1):
    import jax
    import jax.numpy as jnp

    def _L0_gnn_ref(x, edge_index, ln_in_g, ln_in_b, W1, b1, W2, b2, layer_Wa, layer_ba, layer_Wb, layer_bb, layer_ng, layer_nb, Wd1, bd1, Wd2, bd2, out_g, out_b):
        import jax, jax.numpy as jnp
        import numpy as np
        N = 6250
        E = 100000
        D_IN = 1024
        D_HID = 512
        D_B = 256
        N_LAYERS = 3
        LN_EPS = 1e-05

        def layernorm(x, g, b):
            m = jnp.mean(x, axis=-1, keepdims=True)
            v = jnp.mean((x - m) ** 2, axis=-1, keepdims=True)
            return (x - m) * jax.lax.rsqrt(v + LN_EPS) * g + b
        n = x.shape[0]
        src, dst = (edge_index[0], edge_index[1])
        h = layernorm(x, ln_in_g, ln_in_b)
        h = jax.nn.relu(h @ W1 + b1)
        h = h @ W2 + b2
        for i in range(N_LAYERS):
            agg = jax.ops.segment_sum(h[src], dst, num_segments=n)
            z = h + agg
            z = jax.nn.relu(z @ layer_Wa[i] + layer_ba[i])
            z = z @ layer_Wb[i] + layer_bb[i]
            z = jax.nn.relu(layernorm(z, layer_ng[i], layer_nb[i]))
            h = h + z
        delta = jax.nn.relu(h @ Wd1 + bd1) @ Wd2 + bd2
        return layernorm(x + delta, out_g, out_b)

    def _L1_gnn_ref(x, edge_src, edge_dst, W_self0, W_neigh0, b0, W_self1, W_neigh1, b1):
        import jax, jax.numpy as jnp
        import numpy as np
        N_NODES = 3125
        N_EDGES = 50000
        D = 1024

        def _sage_layer(h, edge_src, edge_dst, deg_inv, W_self, W_neigh, b):
            msg = h[edge_src]
            agg = jax.ops.segment_sum(msg, edge_dst, num_segments=h.shape[0])
            mean = agg * deg_inv[:, None]
            return h @ W_self + mean @ W_neigh + b
        N = x.shape[0]
        deg = jax.ops.segment_sum(jnp.ones_like(edge_dst, dtype=x.dtype), edge_dst, num_segments=N)
        deg_inv = 1.0 / jnp.maximum(deg, 1.0)
        h = jax.nn.relu(_sage_layer(x, edge_src, edge_dst, deg_inv, W_self0, W_neigh0, b0))
        out = _sage_layer(h, edge_src, edge_dst, deg_inv, W_self1, W_neigh1, b1)
        return out
    edge_index = jnp.stack([src, dst])
    x = _layernorm(x + _L0_gnn_ref(x, edge_index, L0_gnn_ln_in_g, L0_gnn_ln_in_b, L0_gnn_W1, L0_gnn_b1, L0_gnn_W2, L0_gnn_b2, L0_gnn_layer_Wa, L0_gnn_layer_ba, L0_gnn_layer_Wb, L0_gnn_layer_bb, L0_gnn_layer_ng, L0_gnn_layer_nb, L0_gnn_Wd1, L0_gnn_bd1, L0_gnn_Wd2, L0_gnn_bd2, L0_gnn_out_g, L0_gnn_out_b), axis=-1)
    x = _layernorm(x + _L1_gnn_ref(x, src, dst, L1_gnn_W_self0, L1_gnn_W_neigh0, L1_gnn_b0, L1_gnn_W_self1, L1_gnn_W_neigh1, L1_gnn_b1), axis=-1)
    return x

_drawn_inputs = setup_inputs


def setup_inputs(seed=0):
    import zlib

    import numpy as np

    out = dict(_drawn_inputs(seed))
    spreads = {'L0_gnn_ln_in_g': (1.0, 0.6),
     'L0_gnn_ln_in_b': (0.0, 0.8),
     'L0_gnn_b1': (0.0, 2.0),
     'L0_gnn_b2': (0.0, 0.967),
     'L0_gnn_layer_ba': (0.0, 2.0),
     'L0_gnn_layer_bb': (0.0, 1.793),
     'L0_gnn_layer_ng': (1.0, 0.6),
     'L0_gnn_layer_nb': (0.0, 0.8),
     'L0_gnn_bd1': (0.0, 0.425),
     'L0_gnn_bd2': (0.0, 0.1),
     'L0_gnn_out_g': (1.0, 0.2),
     'L0_gnn_out_b': (0.0, 0.1),
     'L1_gnn_b0': (0.0, 0.1),
     'L1_gnn_b1': (0.0, 0.1)}
    factors = {'L0_gnn_W1': 4.994}
    for name, (base, spread) in spreads.items():
        noise = np.random.default_rng([zlib.crc32(name.encode()), seed]).standard_normal(out[name].shape)
        drawn = base * np.exp(spread * noise) if base else spread * noise
        out[name] = jnp.asarray(drawn.astype(out[name].dtype))
    for name, factor in factors.items():
        out[name] = (out[name] * factor).astype(out[name].dtype)
    return out
```

```python
import concourse.bass as bass
from concourse import mybir

ALU = mybir.AluOpType
ACT = mybir.ActivationFunctionType
AX = mybir.AxisListType
F32 = mybir.dt.float32
F32R = mybir.dt.float32r
BF16 = mybir.dt.bfloat16
F16 = mybir.dt.float16
I32 = mybir.dt.int32

N, E = 1250, 20000
D, H, B, LAYERS = 1024, 512, 256, 3
NT = 125
T = N // NT
EC = 125
C = E // EC
Q = C // 2
KD, KH, KB = D // 128, H // 128, B // 128
CH = 418
NCH = -(-N // CH)
NW = CH * NCH
EPS = 1e-5
HALVES = ((0, 0), (0, 1), (1, 0))


def raw(ap):
    return ap.bitcast(F32)


class Map:

    def __init__(self, nc, start):
        self.nc, self.at = nc, start

    def __call__(self, name, shape, dt):
        size = 2 if dt in (BF16, F16) else 4
        for n in shape[1:]:
            size *= n
        t = self.nc.alloc_sbuf_tensor_at(name, list(shape), dt, offset=self.at)
        self.at += -(-size // 32) * 32
        return t


def newton_rstd(dve, done, count, rstd, var_eps, root, scratch):
    dve.reciprocal(rstd, root).then_inc(done, 1)
    dve.wait_ge(done, count + 1)
    dve.tensor_tensor(scratch, rstd, rstd, ALU.mult).then_inc(done, 1)
    dve.wait_ge(done, count + 2)
    dve.tensor_tensor(scratch, scratch, var_eps, ALU.mult).then_inc(done, 1)
    dve.wait_ge(done, count + 3)
    dve.tensor_scalar(scratch, scratch, -0.5, 1.5, ALU.mult, ALU.add).then_inc(done, 1)
    dve.wait_ge(done, count + 4)
    dve.tensor_tensor(rstd, rstd, scratch, ALU.mult).then_inc(done, 1)
    dve.wait_ge(done, count + 5)


def carry_waits(eng, carried):
    eng.sem_inc(carried, 1)


def norm_stats(dve, step, count, stats, mean_var, var_eps, var_ready, halves, carried):
    for h, half in enumerate(halves):
        dve.bn_stats(stats[:, h, :], half).then_inc(step, 1)
    dve.wait_ge(step, count + len(halves))
    carry_waits(dve, carried)
    dve.bn_aggr(mean_var, stats).then_inc(step, 1)
    dve.wait_ge(step, count + len(halves) + 1)
    dve.tensor_scalar(var_eps, mean_var[:, 1:2], EPS, None, ALU.add).then_inc(var_ready, 1)


def norm_shift(dve, shift, mean_var, rstd, norm_ready):
    dve.scalar_tensor_tensor(out=shift, in0=mean_var[:, 0:1], scalar=-1.0, in1=rstd,
                             op0=ALU.mult, op1=ALU.mult).then_inc(norm_ready, 1)


def graph_block(nc, block, sem, io, s):
    RING = 4
    edges_in, weights_in, consts_in = sem("edges_in"), sem("pair_weights_in"), sem("consts_in")
    x_in = [sem("x_in0"), sem("x_in1")]
    rng_step, range_part, range_cols, range_back, ranges = (sem("rng_step"), sem("range_part"),
        sem("range_cols"), sem("range_back"), sem("ranges"))
    range_col_max = sem("range_col_max")
    hot_ready, hot_free = sem("hot_ready"), sem("hot_free")
    counts_done, counts_out = sem("counts_done"), sem("counts_out")
    var_ready, root_ready, norm_ready, dve_step = (sem("var_ready"), sem("root_ready"),
        sem("norm_ready"), sem("dve_step"))
    xhat_ready, xhat_read, xt_affine, xt_hi, xt_split = (sem("xhat_ready"), sem("xhat_read"),
        sem("xt_affine"), sem("xt_hi"), sem("xt_split"))
    at_turned, at_out, at_eye = sem("at_turned"), sem("at_out"), sem("at_eye")
    at_stored, at_placed, eye_placed = [[sem(f"{n}{u}") for u in range(2)]
                                        for n in ("at_stored", "at_placed", "eye_placed")]
    w_in, w_hi, w_ready = sem("gw_in"), sem("gw_hi"), sem("gw_ready")
    zeroed, deg_step = sem("zeroed"), sem("deg_step")

    at = Map(nc, s.wide_at)
    hot_at = at.at
    hot_src = [at(f"hot_src{h}", [128, RING, N], BF16) for h in range(2)]
    hot_dst = [at(f"hot_dst{h}", [128, RING, 128], BF16) for h in range(2)]
    iota = at("iota", [128, NW], F16)
    zeros = at("zeros", [128, 128], BF16)
    counts = [at(f"counts{u}", [128, N], F32) for u in range(2)]
    at_stage1 = at("at_stage1", [128, T, NT], F32)
    assert at.at <= s.wide_end, at.at - s.wide_end
    at = Map(nc, hot_at)
    src_i, dst_i = at("src_i", [128, C], I32), at("dst_i", [128, C], I32)
    pair_weights = at("pair_weights", [128, 2, C], F32)
    weighted = at("weighted", [128, 2 * T, C], F32)
    at = Map(nc, s.stage_at)
    src_f, dst_f = at("src_f", [128, C], F32), at("dst_f", [128, C], F32)
    part_max = at("part_max", [128, 2 * T], F32)
    col_max = at("col_max", [128, 1], F32)
    row = at("row", [128, 6 * T], F32)
    ranges_i = at("ranges_i", [128, 3 * T], I32)
    x_rows = [at(f"x_rows{u}", [128, D], F32) for u in range(2)]
    xhat = at("xhat", [128, D], F32)
    stats = at("stats", [128, 2, 6], F32)
    mean_var = [at(f"mean_var{u}", [128, 2], F32) for u in range(2)]
    var_eps, root, rstd, shift = [[at(f"{n}{u}", [128, 1], F32) for u in range(2)]
                                  for n in ("var_eps", "root", "rstd", "shift")]
    scratch = at("scratch", [128, 1], F32)
    deg_part = at("deg_part", [128, 3, T], F32)
    xt_f32 = at("xt_f32", [128, KD, NT], F32)
    s.turned_at = at.at
    eye_block = [at(f"eye_block{u}", [128, NT], F32) for u in range(2)]
    at_stage = [at("at_stage0", [128, T, NT], F32), at_stage1]
    assert at.at <= nc.sbuf_usable_end, at.at - nc.sbuf_usable_end
    w_f32 = nc.alloc_sbuf_tensor_at("w_first", [128, 1024], F32, offset=s.turned_at + 1024)

    ps_counts, ps_x, ps_a = s.banks[0:3], s.banks[3:5], s.banks[5:8]
    COLS = [(0, 418), (418, 834), (834, N)]
    A_GROUPS = [(0, 4), (4, 8), (8, 10)]

    def load_range(eng, t):
        return (eng.value_load(ranges_i[0:1, bass.ds(t, 1)], min_val=0, max_val=Q - 1),
                eng.value_load(ranges_i[0:1, bass.ds(T + t, 1)], min_val=1, max_val=Q),
                eng.value_load(ranges_i[0:1, bass.ds(2 * T + t, 1)], min_val=1, max_val=Q * (T + 1)))

    @block.sync
    def _(sp):
        sp.dma_start(dst_i[0:EC, :], io["dst_t"]).then_inc(edges_in, 16)
        sp.dma_start(src_i[0:EC, :], io["src_t"]).then_inc(edges_in, 16)
        sp.dma_start(pair_weights[0:EC, :, :], io["pair_weights"]).then_inc(weights_in, 16)
        for to, name in ((iota[0:EC, :], "iota"), (s.ident[:, :], "ident"), (s.ln_gb[:, :, :], "ln_gb")):
            sp.dma_start(to, io[name]).then_inc(consts_in, 16)
        for u in range(2):
            sp.dma_start(x_rows[u][0:NT, :], io["x"][u * NT:(u + 1) * NT, :]).then_inc(x_in[u], 16)
        for n in range(2):
            if n:
                sp.wait_ge(w_ready, n)
            sp.dma_start(w_f32[:, :], io["w_units"][n, :, :]).then_inc(w_in, 16)

        def send_turned(i, u):
            t = 2 * i + u
            sp.wait_ge(at_out, 3 * t + 6)
            sp.dma_start(io["at_dram"][bass.ds(t, 1), :, :, :].rearrange("a p k d -> p (a k) d"),
                         at_stage[u][0:NT, :, :]).then_inc(at_stored[u], 16)
            sp.dma_start(raw(s.at_[0:NT, :, bass.ds(t * NT, NT)]), at_stage[u][0:NT, :, :]).then_inc(at_placed[u], 16)

        def send_eye(i, u):
            t = 2 * i + u
            sp.wait_ge(at_placed[u], 16 * i + 32)
            carry_waits(sp, s.carried)
            sp.wait_ge(at_eye, t + 3)
            sp.dma_start(raw(s.at_[0:NT, bass.ds(t, 1), bass.ds(t * NT, NT)]).rearrange("p a n -> p (a n)"),
                         eye_block[u][0:NT, :]).then_inc(eye_placed[u], 16)

        send_turned(0, 0)
        with sp.Fori(0, T // 2 - 1) as i:
            send_turned(i, 1)
            send_eye(i, 0)
            send_turned(i + 1, 0)
            send_eye(i, 1)
        send_turned(T // 2 - 1, 1)
        for u in range(2):
            send_eye(T // 2 - 1, u)
        s.turned_landed = [(landed[u], 16 * (T // 2 + 1)) for landed in (at_stored, eye_placed) for u in range(2)]

    @block.scalar
    def _(act):
        xt_view = [p[:, 0:4 * NT].rearrange("p (k n) -> p k n", k=4) for p in ps_x]
        at_view = [p[0:NT, 0:4 * NT].rearrange("p (k n) -> p k n", k=4) for p in ps_a]

        def take_root(t, u):
            act.wait_ge(var_ready, t + 1)
            act.activation(root[u][0:NT, :], var_eps[u][0:NT, :], ACT.Sqrt).then_inc(root_ready, 1)

        def norm_tile(i, u, last):
            t = 2 * i + u
            act.wait_ge(norm_ready, t + 1)
            act.wait_ge(x_in[u], 16 * i + 16)
            act.wait_ge(xhat_read, t + 1)
            act.activation(xhat[0:NT, :], x_rows[u][0:NT, :], ACT.Identity, bias=shift[u][0:NT, :],
                           scale=rstd[u][0:NT, :]).then_inc(xhat_ready, 1)
            if not last:
                act.wait_ge(xhat_ready, t + 1)
                act.dma_start(x_rows[u][0:NT, :], io["x"][bass.ds((t + 2) * NT, NT), :]).then_inc(x_in[u], 16)

        def read_counts(i, u):
            t = 2 * i + u
            act.wait_ge(counts_done, t + 1)
            for b, (c0, c1) in enumerate(COLS):
                act.activation(counts[u][0:NT, c0:c1], ps_counts[b][0:NT, 0:c1 - c0], ACT.Identity,
                               accum_out=deg_part[0:NT, b, bass.ds(t, 1)]).then_inc(counts_out, 1)

        def affine(i, u):
            t = 2 * i + u
            act.wait_ge(xt_split, t + 1)
            act.wait_ge(xhat_read, t + 2)
            for k in range(KD):
                act.activation(xt_f32[:, k, :], xt_view[k // 4][:, k % 4, :], ACT.Identity,
                               bias=s.ln_gb[:, 1, k:k + 1], scale=s.ln_gb[:, 0, k:k + 1]).then_inc(xt_affine, 1)

        def stage_turned(i, u):
            t = 2 * i + u
            act.wait_ge(at_turned, t + 1)
            act.wait_ge(at_stored[u], 16 * i + 16)
            act.wait_ge(at_placed[u], 16 * i + 16)
            act.wait_ge(at_eye, t + 1)
            for g, (k0, k1) in enumerate(A_GROUPS):
                act.activation(at_stage[u][0:NT, k0:k1, :], at_view[g][:, 0:k1 - k0, :], ACT.Identity)\
                   .then_inc(at_out, 1)

        for u in range(2):
            act.sem_inc(at_stored[u], 16)
            act.sem_inc(at_placed[u], 16)
        act.wait_ge(consts_in, 48)
        take_root(0, 0)
        norm_tile(0, 0, False)
        take_root(1, 1)
        read_counts(0, 0)
        norm_tile(0, 1, False)
        take_root(2, 0)
        affine(0, 0)
        act.wait_ge(w_ready, 2)

        def tile(i, u, load, ahead):
            t = 2 * i + u
            read_counts(i, u)
            norm_tile(i + u, 1 - u, not load)
            if ahead:
                take_root(t + 2, u)
            affine(i, u)
            stage_turned(i + u - 1, 1 - u)

        tile(0, 1, True, True)
        with act.Fori(1, T // 2 - 2) as i:
            tile(i, 0, True, True)
            tile(i, 1, True, True)
        tile(T // 2 - 2, 0, True, True)
        tile(T // 2 - 2, 1, False, True)
        tile(T // 2 - 1, 0, False, False)
        read_counts(T // 2 - 1, 1)
        affine(T // 2 - 1, 1)
        stage_turned(T // 2 - 1, 0)
        stage_turned(T // 2 - 1, 1)

    @block.gpsimd
    def _(pool):
        pool.memset(zeros[0:EC, :], 0.0).then_inc(zeroed, 1)
        pool.memset(raw(s.at_[:, :, N:NW]), 0.0).then_inc(zeroed, 1)
        for hl in range(2):
            pool.memset(raw(s.xn[:, hl, :, N:NW]), 0.0).then_inc(zeroed, 1)
        for n in range(2):
            pool.wait_ge(w_in, 16 * (n + 1))
            pool.tensor_copy(s.wring[:, n, 0, :], w_f32[:, :]).then_inc(w_hi, 1)
            pool.wait_ge(w_hi, n + 1)
            pool.tensor_tensor(s.wring[:, n, 1, :], w_f32[:, :], raw(s.wring[:, n, 0, :]), ALU.subtract)\
                .then_inc(w_ready, 1)

        def split(t):
            cols = bass.ds(t * NT, NT)
            pool.wait_ge(xt_affine, KD * (t + 2))
            pool.tensor_copy(s.xn[:, 0, :, cols], xt_f32[:, :, :]).then_inc(xt_hi, 1)
            pool.wait_ge(xt_hi, t + 1)
            pool.tensor_tensor(s.xn[:, 1, :, cols], xt_f32[:, :, :], raw(s.xn[:, 0, :, cols]), ALU.subtract)\
                .then_inc(xt_split, 1)

        def add_eye(i, u):
            t = 2 * i + u
            pool.wait_ge(at_out, 3 * t + 6)
            pool.wait_ge(eye_placed[u], 16 * i + 16)
            pool.tensor_tensor(eye_block[u][0:NT, :], at_stage[u][0:NT, bass.ds(t, 1), :].rearrange("p a n -> p (a n)"),
                               s.ident[0:NT, 0:NT], ALU.add).then_inc(at_eye, 1)

        pool.sem_inc(xt_split, 1)
        for u in range(2):
            pool.sem_inc(eye_placed[u], 16)
        pool.sem_inc(at_eye, 2)
        pool.wait_ge(consts_in, 48)
        split(0)
        split(1)
        with pool.Fori(0, T // 2 - 1) as i:
            for u in range(2):
                add_eye(i, u)
                split(2 * i + u + 2)
        for u in range(2):
            add_eye(T // 2 - 1, u)

    @block.vector
    def _(dve):
        def variance(i, u):
            t = 2 * i + u
            dve.wait_ge(x_in[u], 16 * i + 16)
            norm_stats(dve, dve_step, 8 * t, stats[0:NT, :, :], mean_var[u][0:NT, :], var_eps[u][0:NT, :],
                       var_ready, [x_rows[u][0:NT, 512 * h:512 * h + 512] for h in range(2)], s.carried)

        def normalizer(t, u):
            dve.wait_ge(var_ready, t + 1)
            dve.wait_ge(root_ready, t + 1)
            newton_rstd(dve, dve_step, 8 * t + 3, rstd[u][0:NT, :], var_eps[u][0:NT, :],
                        root[u][0:NT, :], scratch[0:NT, :])
            norm_shift(dve, shift[u][0:NT, :], mean_var[u][0:NT, :], rstd[u][0:NT, :], norm_ready)

        def hot(t):
            first, last, before = load_range(dve, t)
            with dve.Fori(first, last) as q:
                step = q + before
                slot = dve.snap(step & (RING - 1))
                dve.wait_ge(hot_free, step)
                for h in range(2):
                    dve.tensor_scalar(hot_src[h][0:EC, bass.ds(slot, 1), 0:N].rearrange("p a n -> p (a n)"),
                                      iota[0:EC, 0:N], src_f[0:EC, bass.ds(2 * q + h, 1)], None, ALU.is_equal)
                    mask = dve.tensor_scalar(hot_dst[h][0:EC, bass.ds(slot, 1), :].rearrange("p a n -> p (a n)"),
                                      iota[0:EC, bass.ds(t * NT, 128)], dst_f[0:EC, bass.ds(2 * q + h, 1)],
                                      None, ALU.is_equal)
                mask.then_inc(hot_ready, 1)

        variance(0, 0)
        dve.wait_ge(edges_in, 32)
        dve.tensor_copy(dst_f[0:EC, :], dst_i[0:EC, :]).then_inc(rng_step, 1)
        dve.tensor_copy(src_f[0:EC, :], src_i[0:EC, :]).then_inc(rng_step, 1)
        dve.wait_ge(rng_step, 2)
        dve.wait_ge(weights_in, 16)
        for t in range(T):
            dve.scalar_tensor_tensor(out=weighted[0:EC, t, :], in0=dst_f[0:EC, :], scalar=float((t + 1) * NT),
                                     in1=pair_weights[0:EC, 0, :], op0=ALU.is_lt, op1=ALU.mult)\
               .then_inc(rng_step, 1)
            dve.scalar_tensor_tensor(out=weighted[0:EC, T + t, :], in0=dst_f[0:EC, :], scalar=float(t * NT),
                                     in1=pair_weights[0:EC, 1, :], op0=ALU.is_ge, op1=ALU.mult)\
               .then_inc(rng_step, 1)
        n = 2 + 2 * T
        dve.wait_ge(rng_step, n)
        dve.tensor_reduce(part_max[0:EC, :], weighted[0:EC, :, :], AX.X, ALU.max).then_inc(range_part, 1)
        dve.wait_ge(range_cols, 1)
        dve.tensor_reduce(col_max[0:2 * T, :], ps_a[0][0:2 * T, 0:EC], AX.X, ALU.max).then_inc(range_col_max, 1)
        dve.wait_ge(range_back, 1)
        up, down, last, first, width, before = [row[0:1, j * T:(j + 1) * T] for j in range(6)]
        dve.tensor_copy(row[0:1, 0:2 * T], ps_a[1][0:1, 0:2 * T]).then_inc(rng_step, 1)
        dve.wait_ge(rng_step, n + 1)
        dve.tensor_scalar(last, up, 1.0, None, ALU.max).then_inc(rng_step, 1)
        dve.tensor_scalar(first, down, -1.0, float(Q), ALU.mult, ALU.add).then_inc(rng_step, 1)
        dve.wait_ge(rng_step, n + 3)
        dve.scalar_tensor_tensor(out=first, in0=last, scalar=-1.0, in1=first, op0=ALU.add, op1=ALU.min)\
           .then_inc(rng_step, 1)
        dve.wait_ge(rng_step, n + 4)
        dve.tensor_tensor(width, last, first, ALU.subtract).then_inc(rng_step, 1)
        dve.memset(row[0:1, 5 * T:5 * T + 1], 0.0).then_inc(rng_step, 1)
        n += 6
        dve.wait_ge(rng_step, n)
        for t in range(1, T):
            dve.tensor_tensor(before[:, t:t + 1], before[:, t - 1:t], width[:, t - 1:t], ALU.add).then_inc(rng_step, 1)
            n += 1
            dve.wait_ge(rng_step, n)
        dve.tensor_copy(ranges_i[0:1, 0:T], first).then_inc(ranges, 1)
        dve.tensor_copy(ranges_i[0:1, T:2 * T], last).then_inc(ranges, 1)
        dve.scalar_tensor_tensor(out=ranges_i[0:1, 2 * T:3 * T], in0=before, scalar=float(Q), in1=first,
                                 op0=ALU.add, op1=ALU.subtract).then_inc(ranges, 1)
        dve.wait_ge(ranges, 3)
        dve.wait_ge(consts_in, 48)
        with dve.Fori(0, T // 2 - 1) as i:
            for u in range(2):
                normalizer(2 * i + u, u)
                variance(i + u, 1 - u)
                hot(2 * i + u)
        normalizer(T - 2, 0)
        variance(T // 2 - 1, 1)
        hot(T - 2)
        normalizer(T - 1, 1)
        hot(T - 1)
        dve.wait_ge(counts_out, 3 * T)
        dve.tensor_tensor(s.deg[0:NT, :], deg_part[0:NT, 0, :], deg_part[0:NT, 1, :], ALU.add).then_inc(deg_step, 1)
        dve.wait_ge(deg_step, 1)
        dve.tensor_tensor(s.deg[0:NT, :], s.deg[0:NT, :], deg_part[0:NT, 2, :], ALU.add).then_inc(deg_step, 1)
        dve.wait_ge(deg_step, 2)
        dve.tensor_scalar(s.deg[0:NT, :], s.deg[0:NT, :], 1.0, None, ALU.max).then_inc(deg_step, 1)
        dve.wait_ge(deg_step, 3)
        dve.reciprocal(s.deg_inv[0:NT, :], s.deg[0:NT, :]).then_inc(deg_step, 1)

    @block.tensor
    def _(pe):
        pe.wait_ge(consts_in, 48)
        pe.wait_ge(range_part, 1)
        pe.transpose(ps_a[0][0:2 * T, 0:EC], part_max[0:EC, :], s.ident[0:EC, 0:EC]).then_inc(range_cols, 1)
        pe.wait_ge(range_col_max, 1)
        pe.matmul(ps_a[1][0:1, 0:2 * T], col_max[0:2 * T, :], s.ident[0:2 * T, 0:2 * T], start=True, stop=True)\
          .then_inc(range_back, 1)
        pe.sem_inc(hot_free, Q + RING - 1)
        pe.sem_inc(hot_ready, Q - 1)
        pe.sem_inc(xhat_read, 1)
        pe.sem_inc(xt_affine, KD)
        pe.sem_inc(at_out, 3)
        pe.wait_ge(ranges, 3)
        pe.wait_ge(zeroed, 4)

        any_finite = iota.bitcast(BF16)

        def count(t):
            first, last, before = load_range(pe, t)
            for b, (c0, c1) in enumerate(COLS):
                pe.matmul(ps_counts[b][:, 0:c1 - c0], zeros[0:EC, :], any_finite[0:EC, 0:c1 - c0],
                          start=True, stop=False)
            with pe.Fori(first, last) as q:
                step = q + before
                slot = pe.snap(step & (RING - 1))
                pe.wait_ge(hot_ready, step)
                for h in range(2):
                    for b, (c0, c1) in enumerate(COLS):
                        mm = pe.matmul(ps_counts[b][:, 0:c1 - c0],
                                       hot_dst[h][0:EC, bass.ds(slot, 1), :].rearrange("p a n -> p (a n)"),
                                       hot_src[h][0:EC, bass.ds(slot, 1), c0:c1].rearrange("p a n -> p (a n)"),
                                       start=False, stop=False)
                mm.then_inc(hot_free, 1)
            for b in range(3):
                mm = pe.matmul(ps_counts[b][:, 0:2], zeros[0:EC, :], any_finite[0:EC, 0:2], start=False, stop=True)
            mm.then_inc(counts_done, 1)

        def turn_norm(t):
            pe.wait_ge(xhat_ready, t + 1)
            pe.wait_ge(xt_affine, KD * (t + 1))
            for k in range(KD):
                mm = pe.transpose(ps_x[k // 4][:, (k % 4) * NT:(k % 4 + 1) * NT],
                                  xhat[0:NT, k * 128:(k + 1) * 128], s.ident[0:NT, 0:NT])
            mm.then_inc(xhat_read, 1)

        def turn_counts(t, u):
            pe.wait_ge(counts_out, 3 * t + 3)
            pe.wait_ge(at_out, 3 * t + 3)
            for g, (k0, k1) in enumerate(A_GROUPS):
                for k in range(k0, k1):
                    mm = pe.transpose(ps_a[g][0:NT, (k - k0) * NT:(k - k0 + 1) * NT],
                                      counts[u][0:NT, k * NT:(k + 1) * NT], s.ident[0:NT, 0:NT])
            mm.then_inc(at_turned, 1)

        count(0)
        turn_norm(0)
        with pe.Fori(0, T // 2 - 1) as i:
            for u in range(2):
                pe.wait_ge(counts_out, 3 * (2 * i + u) + 3)
                count(2 * i + u + 1)
                turn_norm(2 * i + u + 1)
                turn_counts(2 * i + u, u)
        pe.wait_ge(counts_out, 3 * (T - 1))
        count(T - 1)
        turn_norm(T - 1)
        turn_counts(T - 2, 0)
        turn_counts(T - 1, 1)


def encoder_block(nc, block, sem, io, s):
    w_in, w_hi, w_ready, w_free = sem("w_in"), sem("w_hi"), sem("w_ready"), sem("w_free")
    wd_in = [sem(f"wd_in{k}") for k in range(3)]
    wd_hi, wd_ready = sem("wd_hi"), sem("wd_ready")
    vec_in = sem("vec_in")
    z_mm, z_out, z_hi, z_split = sem("z_mm"), sem("z_out"), sem("z_hi"), sem("z_split")
    g_mm, g_hi, g_lo = sem("g_mm"), sem("g_hi"), sem("g_lo")
    b_mm, b_added, b_step, b_root, b_norm = (sem("b_mm"), sem("b_added"), sem("b_step"), sem("b_root"),
        sem("b_norm"))
    b_stats, b_var = sem("b_stats"), sem("b_var")
    t_mm, t_out, h_added, h_hi, h_ready = sem("t_mm"), sem("t_out"), sem("h_added"), sem("h_hi"), sem("h_ready")

    at = Map(nc, s.stage_at)
    w_f32 = at("w_f32", [128, 1024], F32)
    act_out = [at(f"act_out{u}", [128, CH], F32) for u in range(2)]
    bb_row = at("bb_row", [128, LAYERS, B], F32)
    b_mv = at("b_mv", [128, T, 2], F32)
    b_ve, b_rt, b_rs, b_scr = [at(f"b_{n}", [128, T], F32) for n in ("ve", "rt", "rs", "scr")]
    b_st = at("b_st", [128, T, 6], F32)
    z_new = [at(f"z_new{u}", [128, KB, NT], F32) for u in range(2)]
    assert at.at <= s.turned_at, at.at - s.turned_at
    zb = at("zb", [128, T, B], F32)
    assert at.at <= nc.sbuf_usable_end, at.at - nc.sbuf_usable_end
    at = Map(nc, s.xn_at)
    ht = at("ht", [128, 2, KB, NW], F32R)
    zt = at("zt", [128, 2, KB, NW], F32R)
    gn = at("gn", [128, 2, T, B], F32R)
    h_f32 = at("h_f32", [128, KB, NW], F32)
    wd_f32 = [at(f"wd_f32_{u}", [128, D], F32) for u in range(2)] + [w_f32]
    assert at.at <= s.ring_at, at.at - s.ring_at

    ps_z, ps_g, ps_t = s.banks[0:2], s.banks[2:6], s.banks[6:8]

    B1, B2, BA, NG, NB, BD = 0, KH, KH + KB, KH + KB + KB * LAYERS, KH + KB + 2 * KB * LAYERS, KH + KB + 3 * KB * LAYERS
    UNIT_W2, UNIT_WA, UNIT_B0, UNIT_WD1, UNIT_B1 = KH, KH + 1, KH + 2, KH + 3, KH + 4
    UNITS = UNIT_B1 + LAYERS - 1
    SLOT = [0, 1, 0, 1, 0, 1, 0, 1, 0]
    FREED = [0, 0, 1, 2, 3, 4, 5, 6, 7]
    ZC = KB * NCH
    TILES = [0] + [min(T, (c + 1) * CH // NT) for c in range(NCH)]
    EARLY = TILES[NCH - 1]
    AHEAD = 4
    GROUPS = ((0, EARLY), (EARLY, T))
    Z0 = (KH + KB) * NCH
    ZD = Z0 + ZC * LAYERS

    def chunk(j):
        return j % KB, slice((j // KB) * CH, (j // KB + 1) * CH)

    def over_layers(eng, layer):
        with eng.Fori(0, LAYERS - 1) as i:
            layer(i, False)
        layer(LAYERS - 1, True)

    def nodes(t):
        return slice(t * NT, (t + 1) * NT)

    @block.sync
    def _(sp):
        sp.dma_start(s.biases[:, :], io["biases"]).then_inc(vec_in, 16)
        for i in range(LAYERS):
            sp.dma_start(bb_row[0:NT, i, :], io["bb"][i:i + 1, :].to_broadcast([NT, B])).then_inc(vec_in, 16)
        for n in range(2, UNITS):
            if n >= 3:
                sp.wait_ge(w_ready, n)
            sp.dma_start(w_f32[:, :], io["w_units"][n, :, :]).then_inc(w_in, 16)
            if n == UNIT_WD1:
                sp.wait_ge(z_mm, KH * NCH)
                for k in range(2):
                    sp.dma_start(wd_f32[k][:, :], io["Wd2"][k * 128:(k + 1) * 128, :]).then_inc(wd_in[k], 16)
        sp.wait_ge(w_ready, UNITS)
        sp.dma_start(w_f32[:, :], io["Wd2"][2 * 128:3 * 128, :]).then_inc(wd_in[2], 16)
        sp.wait_ge(wd_ready, 1)
        sp.dma_start(wd_f32[0][:, :], io["Wd2"][3 * 128:4 * 128, :]).then_inc(wd_in[0], 16)

    @block.gpsimd
    def _(pool):
        def halves(n, slot):
            pool.wait_ge(w_in, 16 * (n + 1))
            carry_waits(pool, s.carried)
            pool.tensor_copy(s.wring[:, slot, 0, :], w_f32[:, :]).then_inc(w_hi, 1)
            pool.wait_ge(w_hi, n + 1)
            pool.tensor_tensor(s.wring[:, slot, 1, :], w_f32[:, :], raw(s.wring[:, slot, 0, :]), ALU.subtract)\
                .then_inc(w_ready, 1)

        def layer(i, last):
            for t in range(T):
                pool.wait_ge(t_out, KB * (T * i + t + 1))
                pool.tensor_tensor(h_f32[:, :, nodes(t)], h_f32[:, :, nodes(t)], z_new[t % 2][:, :, :], ALU.add)\
                    .then_inc(h_added, 1)
            if not last:
                pool.wait_ge(w_free, FREED[UNIT_B1] + i)
                halves(UNIT_B1 + i, SLOT[UNIT_B1])

        pool.sem_inc(w_in, 32)
        pool.sem_inc(w_hi, 2)
        pool.sem_inc(w_ready, 2)
        pool.sem_inc(h_added, 2)
        for n in range(2, UNIT_B1):
            pool.wait_ge(w_free, FREED[n])
            halves(n, SLOT[n])
        over_layers(pool, layer)
        for k in range(KH):
            hi, lo = [s.w_self[:, h, k * D:(k + 1) * D] for h in range(2)]
            pool.wait_ge(wd_hi, k + 1)
            pool.tensor_tensor(lo, wd_f32[k % 3][:, :], raw(hi), ALU.subtract).then_inc(wd_ready, 1)

    @block.scalar
    def _(act):
        def relu(n, j, bias):
            act.wait_ge(z_mm, n + 1)
            act.wait_ge(z_split, n + 1)
            carry_waits(act, s.carried)
            act.activation(act_out[j % 2][:, :], ps_z[j % 2][:, 0:CH], ACT.Relu,
                           bias=s.biases[:, bass.ds(bias, 1)]).then_inc(z_out, 1)

        def g_high(i, t):
            act.wait_ge(g_mm, T * i + t + 1)
            act.activation(gn[0:NT, 0, t, :], ps_g[t % 4][0:NT, 0:B], ACT.Copy).then_inc(g_hi, 1)

        def h_high(i, t):
            act.wait_ge(h_added, T * i + t + 3)
            act.activation(ht[:, 0, :, nodes(t)], h_f32[:, :, nodes(t)], ACT.Copy).then_inc(h_hi, 1)

        def turned(i, t):
            act.wait_ge(t_mm, T * i + t + 1)
            act.wait_ge(h_added, T * i + t + 1)
            carry_waits(act, s.carried)
            for k in range(KB):
                act.activation(z_new[t % 2][:, k, :], ps_t[t % 2][:, k * NT:(k + 1) * NT], ACT.Relu,
                               bias=s.biases[:, bass.ds(NB + KB * i + k, 1)],
                               scale=s.biases[:, bass.ds(NG + KB * i + k, 1)]).then_inc(t_out, 1)

        def roots(i, group):
            lo, hi = GROUPS[group]
            act.wait_ge(b_var, 2 * i + group + 1)
            act.activation(b_rt[0:NT, lo:hi], b_ve[0:NT, lo:hi], ACT.Sqrt).then_inc(b_root, 1)

        def update(i, lo, hi, between):
            for t in range(lo, hi):
                turned(i, t)
                if t >= lo + 2:
                    h_high(i, t - 2)
            for t in range(hi - 2, hi):
                between(t)
                h_high(i, t)

        def wd2_high(k):
            hi = s.w_self[:, 0, k * D:(k + 1) * D]
            act.wait_ge(wd_in[k % 3], 16 * (k // 3 + 1))
            act.activation(hi, wd_f32[k % 3][:, :], ACT.Copy).then_inc(wd_hi, 1)

        def layer(i, last):
            for j in range(ZC):
                if j == ZC - 1:
                    roots(i, 0)
                relu(Z0 + ZC * i + j, j, BA + KB * i + j % KB)
            update(i, 0, EARLY, lambda t: None)
            roots(i, 1)
            if last:
                for j in range(KH):
                    relu(ZD + j, j, BD + j)
                update(i, EARLY, T, lambda t: None)
                return
            for t in range(AHEAD):
                g_high(i + 1, t)
            update(i, EARLY, T, lambda t: g_high(i + 1, t - (T - 2) + AHEAD))
            for t in range(AHEAD + 2, T):
                g_high(i + 1, t)

        act.wait_ge(vec_in, 16 * (1 + LAYERS))
        with act.Fori(0, KH // 2) as i:
            for j in range(2 * NCH):
                relu(2 * NCH * i + j, j, B1 + 2 * i + j // NCH)
        for j in range(ZC):
            act.wait_ge(z_mm, KH * NCH + j + 1)
            k, cols = chunk(j)
            act.activation(h_f32[:, k, cols], ps_z[j % 2][:, 0:CH], ACT.Identity,
                           bias=s.biases[:, B2 + k:B2 + k + 1]).then_inc(z_out, 1)
        for t in range(T):
            g_high(0, t)
        over_layers(act, layer)
        for j in range(KH, KH * NCH):
            if j % 2 == 0:
                wd2_high((j - KH) // 2)
            relu(ZD + j, j, BD + j % KH)

    @block.vector
    def _(dve):
        def split(n, dst_hi, dst_lo, src):
            dve.wait_ge(z_out, n + 1)
            dve.tensor_copy(dst_hi, src).then_inc(z_hi, 1)
            dve.wait_ge(z_hi, n + 1)
            dve.tensor_tensor(dst_lo, src, raw(dst_hi), ALU.subtract).then_inc(z_split, 1)

        def g_low(i, t):
            dve.wait_ge(g_hi, T * i + t + 1)
            dve.tensor_tensor(gn[0:NT, 1, t, :], ps_g[t % 4][0:NT, 0:B], raw(gn[0:NT, 0, t, :]),
                              ALU.subtract).then_inc(g_lo, 1)

        def h_low(i, t):
            dve.wait_ge(h_hi, T * i + t + 1)
            dve.tensor_tensor(ht[:, 1, :, nodes(t)], h_f32[:, :, nodes(t)], raw(ht[:, 0, :, nodes(t)]),
                              ALU.subtract).then_inc(h_ready, 1)

        def add_bias(i, t):
            dve.wait_ge(b_mm, T * i + t + 1)
            dve.tensor_tensor(zb[0:NT, t, :], ps_g[2 + t % 2][0:NT, 0:B],
                              bb_row[0:NT, bass.ds(i, 1), :].rearrange("p a n -> p (a n)"), ALU.add)\
               .then_inc(b_added, 1)
            dve.wait_ge(b_added, T * i + t + 1)
            dve.bn_stats(b_st[0:NT, t, :], zb[0:NT, t, :]).then_inc(b_stats, 1)

        def variances(i, group):
            lo, hi = GROUPS[group]
            dve.wait_ge(b_stats, T * i + hi)
            carry_waits(dve, s.carried)
            for t in range(lo, hi):
                dve.bn_aggr(b_mv[0:NT, t, :], b_st[0:NT, t, :]).then_inc(b_step, 1)
            dve.wait_ge(b_step, (T + 10) * i + hi + 5 * group)
            dve.tensor_scalar(b_ve[0:NT, lo:hi], b_mv[0:NT, lo:hi, 1], EPS, None, ALU.add).then_inc(b_var, 1)

        def normalize(i, group):
            lo, hi = GROUPS[group]
            dve.wait_ge(b_var, 2 * i + group + 1)
            dve.wait_ge(b_root, 2 * i + group + 1)
            newton_rstd(dve, b_step, (T + 10) * i + hi + 5 * group, b_rs[0:NT, lo:hi], b_ve[0:NT, lo:hi],
                        b_rt[0:NT, lo:hi], b_scr[0:NT, lo:hi])
            for t in range(lo, hi):
                dve.tensor_scalar(zb[0:NT, t, :], zb[0:NT, t, :], b_mv[0:NT, t, 0:1], b_rs[0:NT, t:t + 1],
                                  ALU.subtract, ALU.mult).then_inc(b_norm, 1)

        def layer(i, last):
            for j in range(ZC):
                k, cols = chunk(j)
                if j == ZC - 1:
                    variances(i, 0)
                    normalize(i, 0)
                split(Z0 + ZC * i + j, zt[:, 0, k, cols], zt[:, 1, k, cols], act_out[j % 2][:, :])
                if j >= KB and j % KB == 0:
                    for t in range(TILES[j // KB - 1], TILES[j // KB]):
                        add_bias(i, t)
            for t in range(EARLY, T):
                add_bias(i, t)
                h_low(i, t - EARLY)
            variances(i, 1)
            for t in range(T - EARLY, EARLY):
                h_low(i, t)
            normalize(i, 1)
            if last:
                for j in range(KH):
                    split_wide(j)
                for t in range(EARLY, T):
                    h_low(i, t)
                return
            for t in range(AHEAD):
                g_low(i + 1, t)
            for t in range(EARLY, T):
                if t == T - 1:
                    g_low(i + 1, AHEAD)
                h_low(i, t)
            for t in range(AHEAD + 1, T):
                g_low(i + 1, t)

        def split_wide(j):
            k, c = j % KH, j // KH
            hi, lo = [s.wide[:, hl, k, c * CH:(c + 1) * CH] for hl in range(2)]
            split(ZD + j, hi, lo, act_out[j % 2][:, :])

        dve.sem_inc(z_split, 2)
        dve.wait_ge(vec_in, 16 * (1 + LAYERS))
        for landed, count in s.turned_landed:
            dve.wait_ge(landed, count)
        with dve.Fori(0, KH // 2) as i:
            for j in range(2 * NCH):
                cols = bass.ds((j % NCH) * CH, CH)
                hi, lo = [s.wide[:, hl, bass.ds(2 * i + j // NCH, 1), cols] for hl in range(2)]
                hi, lo = [x.rearrange("p a n -> p (a n)") for x in (hi, lo)]
                split(2 * NCH * i + j, hi, lo, act_out[j % 2][:, :])
        for j in range(ZC):
            k, cols = chunk(j)
            split(KH * NCH + j, ht[:, 0, k, cols], ht[:, 1, k, cols], h_f32[:, k, cols])
        for t in range(T):
            g_low(0, t)
        over_layers(dve, layer)
        for j in range(KH, KH * NCH):
            split_wide(j)

    @block.tensor
    def _(pe):
        def dense(out, w, x, k_tiles):
            for k in range(k_tiles):
                for p, (a, b) in enumerate(HALVES):
                    mm = pe.matmul(out, w(a, k), x(b, k), start=(k == 0 and p == 0),
                                   stop=(k == k_tiles - 1 and p == 2))
            return mm

        def weights(slot, half):
            return lambda h, k: s.wring[:, slot, h, (half * KB + k) * B:(half * KB + k + 1) * B]

        def g_tile(t, w):
            dense(ps_g[t % 4][0:NT, 0:B], lambda h, k: ht[:, h, k, nodes(t)], w, KB).then_inc(g_mm, 1)

        def next_g(i, lo, hi):
            for t in range(lo, hi):
                pe.wait_ge(h_ready, T * i + t + 1)
                if t < 4:
                    pe.wait_ge(b_added, T * i + T)
                else:
                    pe.wait_ge(g_lo, T * (i + 1) + t - 3)
                g_tile(t, weights(SLOT[UNIT_B0], 1))

        def with_counts(i, j):
            m, cols = chunk(j)
            pe.wait_ge(z_split, Z0 + ZC * i + j + 1)
            for k in range(T):
                for h in range(2):
                    mm = pe.matmul(ps_z[j % 2][:, 0:CH], gn[0:NT, h, k, m * 128:(m + 1) * 128],
                                   s.at_[0:NT, k, cols], start=(k == 0 and h == 0), stop=(k == T - 1 and h == 1))
            mm.then_inc(z_mm, 1)

        def second(i, c):
            if c == 0:
                pe.wait_ge(w_ready, UNIT_B1 + i)
            pe.wait_ge(z_split, Z0 + ZC * i + KB * (c + 1) + 2)
            for t in range(TILES[c], TILES[c + 1]):
                if t >= 2:
                    pe.wait_ge(b_added, T * i + t - 1)
                mm = dense(ps_g[2 + t % 2][0:NT, 0:B], lambda h, k: zt[:, h, k, nodes(t)],
                           weights(SLOT[UNIT_B0], 0), KB)
                mm.then_inc(b_mm, 1)

        def turn(i, lo, hi):
            for t in range(lo, hi):
                pe.wait_ge(b_norm, T * i + t + 1)
                if t >= 2:
                    pe.wait_ge(t_out, KB * (T * i + t - 1))
                for k in range(KB):
                    mm = pe.transpose(ps_t[t % 2][:, k * NT:(k + 1) * NT], zb[0:NT, t, k * 128:(k + 1) * 128],
                                      s.ident[0:NT, 0:NT])
                mm.then_inc(t_mm, 1)

        def last_dense(c):
            wd1 = s.wring[:, SLOT[UNIT_WD1], :, :].rearrange("p h (k m) -> p h k m", k=KB)
            cols = slice(c * CH, (c + 1) * CH)
            pe.wait_ge(h_ready, T * (LAYERS - 1) + min(T, -(-(c + 1) * CH // NT)))
            for m in range(KH):
                j = KH * c + m
                pe.wait_ge(z_split, ZD + j + 1)
                mm = dense(ps_z[j % 2][:, 0:CH], lambda h, k: wd1[:, h, k, m * 128:(m + 1) * 128],
                           lambda h, k: ht[:, h, k, cols], KB)
                mm.then_inc(z_mm, 1)

        def layer(i, last):
            pe.wait_ge(g_lo, T * i + T)
            for j in range(ZC):
                with_counts(i, j)
                if j >= KB and j % KB == 0:
                    second(i, j // KB - 1)
            turn(i, 0, EARLY)
            second(i, NCH - 1)
            if last:
                last_dense(0)
                turn(i, EARLY, T)
                for c in range(1, NCH):
                    last_dense(c)
                return
            next_g(i, 0, AHEAD)
            turn(i, EARLY, T)
            next_g(i, AHEAD, T)
            pe.wait_ge(g_mm, T * i + 2 * T)
            pe.sem_inc(w_free, 1)

        with pe.Fori(0, KH // 2) as i:
            for u in range(2):
                w = s.wring[:, u, :, :].rearrange("p h (k m) -> p h k m", k=KD)
                pe.wait_ge(w_ready, 2 * i + u + 1)
                for c in range(NCH):
                    j = u * NCH + c
                    cols = slice(c * CH, (c + 1) * CH)
                    pe.wait_ge(z_split, 2 * NCH * i + j + 1)
                    mm = dense(ps_z[j % 2][:, 0:CH], lambda h, k: w[:, h, k, :], lambda h, k: s.xn[:, h, k, cols], KD)
                    mm.then_inc(z_mm, 1)
                pe.wait_ge(z_mm, 2 * NCH * i + (u + 1) * NCH)
                pe.sem_inc(w_free, 1)
        done = KH * NCH
        w2 = s.wring[:, 0, :, :].rearrange("p h (k m) -> p h k m", k=KH)
        pe.wait_ge(w_ready, UNIT_W2 + 1)
        pe.wait_ge(z_split, done + 2)
        for j in range(ZC):
            m, cols = chunk(j)
            if j >= 2:
                pe.wait_ge(z_out, done + j - 1)
            mm = dense(ps_z[j % 2][:, 0:CH], lambda h, k: w2[:, h, k, m * 128:(m + 1) * 128],
                       lambda h, k: s.wide[:, h, k, cols], KH)
            mm.then_inc(z_mm, 1)
        pe.wait_ge(z_mm, done + ZC)
        pe.sem_inc(w_free, 1)
        pe.wait_ge(w_ready, UNIT_WA + 1)
        for t in range(T):
            pe.wait_ge(z_split, done + 2 + KB * (((t + 1) * NT - 1) // CH + 1))
            if t >= 4:
                pe.wait_ge(g_lo, t - 3)
            g_tile(t, weights(SLOT[UNIT_WA], 0))
        pe.wait_ge(g_mm, T)
        pe.sem_inc(w_free, 1)
        for landed, count in s.turned_landed:
            pe.wait_ge(landed, count)
        over_layers(pe, layer)


def decoder_block(nc, block, sem, io, s):
    x_in = [sem("dx_in0"), sem("dx_in1")]
    bd_in, row_in, bias_split, bias_hi, const_set = sem("bd_in"), sem("row_in"), sem("bias_split"), sem("bias_hi"), sem("const_set")
    y_mm, y_added, xo_ready, z1_ready, z2_ready = (sem("y_mm"), sem("y_added"), sem("xo_ready"),
        sem("z1_ready"), sem("z2_ready"))
    mean_ready, sq_ready, root_ready, rstd_step, rstd_ready = [[sem(f"dec_{n}{j}") for j in range(2)]
        for n in ("mean_ready", "sq_ready", "root_ready", "rstd_step", "rstd_ready")]
    shift_ready, x2_ready = sem("shift_ready"), sem("x2_ready")
    x2_out = [sem("x2_out0"), sem("x2_out1")]
    wn_in, wn_hi, wn_ready = [sem("wn_in0"), sem("wn_in1")], sem("wn_hi"), sem("wn_ready")

    at = Map(nc, s.late_at)
    gain_row, bias_row = at("gain_row", [128, D], F32), at("bias_row", [128, D], F32)
    bd_f32 = at("bd_f32", [128, D], F32)
    bd = at("bd", [128, 2, D], F32R)
    ones = at("ones", [128, 128], F32R)
    ones_f32 = at("ones_f32", [128, 128], F32)
    eps = at("eps", [128, 1], F32)
    xr, xo, y, z = [[at(f"{n}{u}", [128, D], F32) for u in range(2)]
                    for n in ("dec_x", "dec_xo", "dec_y", "dec_z")]
    squares = at("squares", [128, D], F32)
    y_sum = [at(f"y_sum{u}", [128, 2], F32) for u in range(2)]
    z_sum = [at(f"z_sum{u}", [128, 1], F32) for u in range(2)]
    minus_mean, square_sum, var_eps, root, rstd, scratch = [
        [[at(f"dec_{n}{j}{u}", [128, 1], F32) for u in range(2)] for j in range(2)]
        for n in ("minus_mean", "square_sum", "var_eps", "root", "rstd", "scratch")]
    shift = [at(f"dec_shift{u}", [128, 1], F32) for u in range(2)]
    w_f32 = [at(f"wn_f32_{u}", [128, 512], F32) for u in range(2)]
    end = nc.sbuf_usable_end - nc.sbuf_usable_end % 32 - 2 * 4 * D
    assert at.at <= end, at.at - end
    at = Map(nc, end)
    x2 = [at(f"dec_x2{u}", [128, D], F32) for u in range(2)]
    banks = s.banks

    def by_pairs(eng, tile):
        tile(0, 0, True)
        tile(0, 1, False)
        with eng.Fori(1, T // 2) as i:
            for u in range(2):
                tile(i, u, False)

    def before(i, u):
        return (i, 0) if u else (i - 1, 1)

    @block.sync
    def _(sp):
        sp.dma_start(bd_f32[0:1, :], io["bd2"]).then_inc(bd_in, 16)
        for u in range(2):
            sp.dma_start(xr[u][0:NT, :], io["x"][u * NT:(u + 1) * NT, :]).then_inc(x_in[u], 16)
        sp.dma_start(gain_row[0:NT, :], io["out_g"].to_broadcast([NT, D])).then_inc(row_in, 16)
        sp.dma_start(bias_row[0:NT, :], io["out_b"].to_broadcast([NT, D])).then_inc(row_in, 16)

        def store(i, u):
            t = 2 * i + u
            sp.wait_ge(x2_ready, t + 3)
            sp.dma_start(io["x2_dram"][bass.ds(t * NT, NT), :], x2[u][0:NT, :]).then_inc(x2_out[u], 16)

        with sp.Fori(0, T // 2 - 1) as i:
            for u in range(2):
                t = 2 * i + u
                sp.wait_ge(xo_ready, t + 1)
                sp.wait_ge(y_added, 2 * t + 2)
                sp.dma_start(xr[u][0:NT, :], io["x"][bass.ds((t + 2) * NT, NT), :]).then_inc(x_in[u], 16)
                store(i, u)
        for layer in range(2):
            sp.dma_start(s.sage_bias[0:NT, layer, :], io["sage_b"][layer:layer + 1, :].to_broadcast([NT, D]))\
              .then_inc(s.bias_in, 16)
        for u in range(2):
            sp.wait_ge(x2_out[u], 48)
            sp.dma_start(s.rows[u][0:NT, :], io["x2_dram"][u * NT:(u + 1) * NT, :]).then_inc(s.rows_in[u], 16)
        for u in range(2):
            store(T // 2 - 1, u)
        s.x2_landed = [(x2_out[u], 16 * (T // 2 + 1)) for u in range(2)]

    @block.gpsimd
    def _(pool):
        pool.memset(ones_f32[:, :], 1.0).then_inc(const_set, 1)
        pool.memset(eps[:, :], EPS).then_inc(const_set, 1)
        pool.wait_ge(const_set, 2)
        pool.tensor_copy(ones[:, :], ones_f32[:, :]).then_inc(const_set, 1)
        for u in range(2):
            pool.dma_start(w_f32[u][:, :], io["w_neigh"][0, 0, u]).then_inc(wn_in[u], 16)
        pool.wait_ge(row_in, 32)
        for t in range(T):
            i, u = divmod(t, 2)
            pool.wait_ge(x_in[u], 16 * i + 16)
            if t >= 2:
                pool.wait_ge(z2_ready, t - 1)
            pool.tensor_tensor(xo[u][0:NT, :], xr[u][0:NT, :], bias_row[0:NT, :], ALU.add).then_inc(xo_ready, 1)
            if t < KD:
                pool.wait_ge(wn_in[u], 16 * i + 16)
                hi, lo = [s.w_neigh[:, h, t * 512:(t + 1) * 512] for h in range(2)]
                pool.tensor_copy(hi, w_f32[u][:, :]).then_inc(wn_hi, 1)
                pool.wait_ge(wn_hi, t + 1)
                pool.tensor_tensor(lo, w_f32[u][:, :], raw(hi), ALU.subtract).then_inc(wn_ready, 1)
                if t + 2 < KD:
                    pool.wait_ge(wn_ready, t + 1)
                    pool.dma_start(w_f32[u][:, :], io["w_neigh"][0, 0, t + 2]).then_inc(wn_in[u], 16)

    @block.scalar
    def _(act):
        def deviations(i, u, j):
            t = 2 * i + u
            act.wait_ge(mean_ready[j], t + 1)
            act.activation(squares[0:NT, :], (z if j else y)[u][0:NT, :], ACT.Square,
                           bias=minus_mean[j][u][0:NT, :], accum_out=square_sum[j][u][0:NT, :]).then_inc(sq_ready[j], 1)
            act.wait_ge(sq_ready[j], t + 1)
            act.activation(root[j][u][0:NT, :], square_sum[j][u][0:NT, :], ACT.Sqrt, bias=eps[0:NT, :],
                           scale=1.0 / D).then_inc(root_ready[j], 1)

        def normalize(i, u):
            act.wait_ge(shift_ready, 2 * i + u + 1)
            act.wait_ge(x2_out[u], 16 * i + 16)
            act.activation(x2[u][0:NT, :], z[u][0:NT, :], ACT.Identity, bias=shift[u][0:NT, :],
                           scale=rstd[1][u][0:NT, :]).then_inc(x2_ready, 1)

        def tile(i, u, first):
            deviations(i, u, 0)
            if not first:
                normalize(*before(i, u))
            deviations(i, u, 1)

        for u in range(2):
            act.sem_inc(x2_out[u], 16)
        act.wait_ge(const_set, 2)
        by_pairs(act, tile)
        normalize(T // 2 - 1, 1)

    @block.vector
    def _(dve):
        def rstds(i, u, j):
            t = 2 * i + u
            ve, rs, sc = var_eps[j][u][0:NT, :], rstd[j][u][0:NT, :], scratch[j][u][0:NT, :]
            dve.wait_ge(sq_ready[j], t + 1)
            dve.tensor_scalar(ve, square_sum[j][u][0:NT, :], 1.0 / D, EPS, ALU.mult, ALU.add).then_inc(rstd_step[j], 1)
            dve.wait_ge(root_ready[j], t + 1)
            dve.reciprocal(rs, root[j][u][0:NT, :]).then_inc(rstd_step[j], 1)
            dve.wait_ge(rstd_step[j], 4 * t + 2)
            dve.scalar_tensor_tensor(out=sc, in0=rs, scalar=ve, in1=rs, op0=ALU.mult, op1=ALU.mult)\
               .then_inc(rstd_step[j], 1)
            dve.wait_ge(rstd_step[j], 4 * t + 3)
            dve.tensor_scalar(sc, sc, -0.5, 1.5, ALU.mult, ALU.add).then_inc(rstd_step[j], 1)
            dve.wait_ge(rstd_step[j], 4 * t + 4)
            dve.tensor_tensor(rs, rs, sc, ALU.mult).then_inc(rstd_ready[j], 1)
            dve.wait_ge(rstd_ready[j], t + 1)

        def second_rstd(i, u):
            rstds(i, u, 1)
            dve.tensor_tensor(shift[u][0:NT, :], minus_mean[1][u][0:NT, :], rstd[1][u][0:NT, :], ALU.mult)\
               .then_inc(shift_ready, 1)

        def tile(i, u, first):
            t = 2 * i + u
            dve.wait_ge(y_mm, t + 1)
            dve.wait_ge(x_in[u], 16 * i + 16)
            for c in range(2):
                cols = slice(512 * c, 512 * c + 512)
                dve.scalar_tensor_tensor(out=y[u][0:NT, cols], in0=banks[2 * u + c][0:NT, :], scalar=1.0,
                                         in1=xr[u][0:NT, cols], op0=ALU.mult, op1=ALU.add,
                                         accum_out=y_sum[u][0:NT, c:c + 1]).then_inc(y_added, 1)
            dve.wait_ge(y_added, 2 * t + 2)
            dve.tensor_scalar(minus_mean[0][u][0:NT, :], y_sum[u][0:NT, 0:1], y_sum[u][0:NT, 1:2], -1.0 / D,
                              ALU.add, ALU.mult).then_inc(mean_ready[0], 1)
            if not first:
                second_rstd(*before(i, u))
            dve.wait_ge(mean_ready[0], t + 1)
            dve.wait_ge(x2_ready, t + 1)
            dve.scalar_tensor_tensor(out=z[u][0:NT, :], in0=y[u][0:NT, :], scalar=minus_mean[0][u][0:NT, :],
                                     in1=gain_row[0:NT, :], op0=ALU.add, op1=ALU.mult).then_inc(z1_ready, 1)
            rstds(i, u, 0)
            dve.wait_ge(z1_ready, t + 1)
            dve.wait_ge(xo_ready, t + 1)
            dve.scalar_tensor_tensor(out=z[u][0:NT, :], in0=z[u][0:NT, :], scalar=rstd[0][u][0:NT, :],
                                     in1=xo[u][0:NT, :], op0=ALU.mult, op1=ALU.add,
                                     accum_out=z_sum[u][0:NT, :]).then_inc(z2_ready, 1)
            dve.wait_ge(z2_ready, t + 1)
            dve.tensor_scalar(minus_mean[1][u][0:NT, :], z_sum[u][0:NT, :], -1.0 / D, None, ALU.mult)\
               .then_inc(mean_ready[1], 1)

        dve.sem_inc(x2_ready, 2)
        dve.wait_ge(bd_in, 16)
        dve.tensor_copy(bd[0:1, 0, :], bd_f32[0:1, :]).then_inc(bias_hi, 1)
        dve.wait_ge(bias_hi, 1)
        dve.tensor_tensor(bd[0:1, 1, :], bd_f32[0:1, :], raw(bd[0:1, 0, :]), ALU.subtract).then_inc(bias_split, 1)
        dve.wait_ge(row_in, 32)
        by_pairs(dve, tile)
        second_rstd(T // 2 - 1, 1)

    @block.tensor
    def _(pe):
        for t in range(T):
            if t >= 2:
                pe.wait_ge(y_added, 2 * (t - 1))
            outs = [banks[2 * (t % 2) + c][0:NT, :] for c in range(2)]
            for c, out in enumerate(outs):
                for k in range(KH):
                    for p, (a, b) in enumerate(HALVES):
                        pe.matmul(out, s.wide[:, a, k, t * NT:(t + 1) * NT],
                                  s.w_self[:, b, k * D + 512 * c:k * D + 512 * c + 512],
                                  start=(k == 0 and p == 0), stop=False)
            if t == 0:
                pe.wait_ge(bias_split, 1)
                pe.wait_ge(const_set, 3)
            for c, out in enumerate(outs):
                for h in range(2):
                    mm = pe.matmul(out, ones[0:1, 0:NT], bd[0:1, h, 512 * c:512 * c + 512],
                                   start=False, stop=(h == 1))
            mm.then_inc(y_mm, 1)


def sage_block(nc, block, sem, io, s):
    rows_in, bias_in, rows, b_rows = s.rows_in, s.bias_in, s.rows, s.sage_bias
    turned, ht_ready, st_hi, st_ready, h_used = (sem("turned"), sem("ht_ready"), sem("st_hi"),
        sem("st_ready"), sem("h_used"))
    g_hi, g_lo = sem("sg_hi"), sem("sg_lo")
    a_in = [sem("a_in0"), sem("a_in1")]
    o_mm, o_biased, o_resid, o_done, o_relu = (sem("o_mm"), sem("o_biased"), sem("o_resid"),
        sem("o_done"), sem("o_relu"))
    o_out = [sem("o_out0"), sem("o_out1")]
    res_in = [sem("res_in0"), sem("res_in1")]
    w_in, w_hi, w_ready = [sem("sw_in0"), sem("sw_in1")], sem("sw_hi"), sem("sw_ready")
    f_step, f_var, f_root, f_norm, f_normed = sem("f_step"), sem("f_var"), sem("f_root"), sem("f_norm"), sem("f_normed")

    g = nc.alloc_sbuf_tensor_at("g_rows", [128, 2, T, 512], F32R, offset=s.g_at)
    at = Map(nc, s.late_at)
    ht = at("h_turned", [128, KD, N], F32)
    st = [at(f"h_stage{u}", [128, 2, KD, NT], F32R) for u in range(2)]
    a_st = [at(f"a_stage{u}", [128, T, NT], F32R) for u in range(2)]
    w_f32 = [at(f"w_stage{u}", [128, 512], F32) for u in range(2)]
    o = [at(f"o{u}", [128, 512], F32) for u in range(2)]
    res = [at(f"res{u}", [128, 2, 512], F32) for u in range(2)]
    f_st = at("f_st", [128, 2, 6], F32)
    f_mv = at("f_mv", [128, 2], F32)
    f_ve, f_rt, f_sc = [at(f"f_{n}", [128, 1], F32) for n in ("ve", "rt", "sc")]
    f_rs, f_sh = [[at(f"f_{n}{u}", [128, 1], F32) for u in range(2)] for n in ("rs", "sh")]
    assert at.at <= nc.sbuf_usable_end, at.at
    ps_t, ps_g, ps_self, ps_a = s.banks[0:2], s.banks[2:4], s.banks[4:6], s.banks[6:8]
    HF = T // 2
    PHASES = [(l, hf, agg) for l in range(2) for hf in range(2) for agg in range(2)]

    def counted(phase):
        return T * phase, T * ((phase + 1) // 2), T * (phase // 2)

    @block.sync
    def _(sp):
        for landed, count in s.x2_landed:
            sp.wait_ge(landed, count)
        for phase, (l, hf, agg) in enumerate(PHASES):
            n0, g0, o0 = counted(phase)
            if not agg and hf == 0:
                src = io["x2_dram"] if l == 0 else io["h1_dram"]
                if l == 1:
                    for u in range(2):
                        sp.wait_ge(o_out[u], 16 * (T + 1))
                    for u in range(2):
                        sp.dma_start(rows[u][0:NT, :], src[u * NT:(u + 1) * NT, :]).then_inc(rows_in[u], 16)
                with sp.Fori(0, HF - 1) as i:
                    for u in range(2):
                        t = 2 * i + u
                        sp.wait_ge(turned, l * T + t + 1)
                        sp.dma_start(rows[u][0:NT, :], src[bass.ds((t + 2) * NT, NT), :]).then_inc(rows_in[u], 16)
            if agg:
                with sp.Fori(0, HF) as i:
                    for u in range(2):
                        t = 2 * i + u
                        sp.wait_ge(o_mm, o0 + t + 1)
                        sp.dma_start(raw(a_st[u][0:NT, :, :]),
                                     io["at_dram"][bass.ds(t, 1), :, :, :].rearrange("a p k d -> p (a k) d"))\
                          .then_inc(a_in[u], 16)
                        if l == 1:
                            sp.wait_ge(o_out[u], 16 * (T + 1) + 16 * HF * hf + 16 * i)
                            sp.dma_start(res[u][0:NT, 0, :], io["x2_dram"][bass.ds(t * NT, NT), 512 * hf:512 * hf + 512])\
                              .then_inc(res_in[u], 16)
                            if hf == 1:
                                sp.dma_start(res[u][0:NT, 1, :], io["y_dram"][bass.ds(t * NT, NT), :]).then_inc(res_in[u], 16)

    @block.gpsimd
    def _(pool):
        for phase, (l, hf, agg) in enumerate(PHASES):
            if phase == 0:
                continue
            w = io["w_self" if agg else "w_neigh"]
            to = s.w_self if agg else s.w_neigh
            for u in range(2):
                pool.dma_start(w_f32[u][:, :], w[l, hf, u]).then_inc(w_in[u], 16)
            if phase >= 2:
                pool.wait_ge(h_used, T * (phase - 1) + 2)
            for k in range(KD):
                u = k % 2
                c = KD * (phase - 1) + k
                hi, lo = [to[:, h, k * 512:(k + 1) * 512] for h in range(2)]
                pool.wait_ge(w_in[u], 16 * (c // 2 + 1))
                pool.tensor_copy(hi, w_f32[u][:, :]).then_inc(w_hi, 1)
                pool.wait_ge(w_hi, c + 1)
                pool.tensor_tensor(lo, w_f32[u][:, :], raw(hi), ALU.subtract).then_inc(w_ready, 1)
                pool.wait_ge(w_ready, c + 1)
                if k + 2 < KD:
                    pool.dma_start(w_f32[u][:, :], w[l, hf, k + 2]).then_inc(w_in[u], 16)

    def through(eng, phase, stage, tile):
        l, hf, agg = PHASES[phase]
        if phase % 4 == 0:
            stage(phase, 0, 0)
        with eng.Fori(0, HF - 1) as i:
            for u in range(2):
                stage(phase, i + u, 1 - u)
                tile(phase, i, u)
        stage(phase, HF - 1, 1)
        tile(phase, HF - 1, 0)
        if phase % 4 != 3:
            stage(phase + 1, 0, 0)
        tile(phase, HF - 1, 1)

    @block.scalar
    def _(act):
        def stage(phase, i, u):
            n0, g0, o0 = counted(phase)
            t = 2 * i + u
            cols = bass.ds(t * NT, NT)
            if phase % 4 == 0:
                l = phase // 4
                act.wait_ge(turned, l * T + t + 1)
                carry_waits(act, s.carried)
                for b in range(2):
                    act.activation(ht[:, 4 * b:4 * b + 4, cols],
                                   ps_t[b][:, 0:4 * NT].rearrange("p (k n) -> p k n", k=4), ACT.Copy)\
                       .then_inc(ht_ready, 1)
                act.wait_ge(ht_ready, 2 * (l * T + t) + 3)
            act.wait_ge(h_used, n0 + t + 1)
            carry_waits(act, s.carried)
            act.activation(st[u][:, 0, :, :], ht[:, :, cols], ACT.Copy).then_inc(st_hi, 1)

        def tile(phase, i, u):
            l, hf, agg = PHASES[phase]
            n0, g0, o0 = counted(phase)
            t = 2 * i + u
            rows_t = bass.ds(t * NT, NT)
            if not agg:
                act.wait_ge(h_used, n0 + t + 3)
                carry_waits(act, s.carried)
                act.activation(g[0:NT, 0, bass.ds(t, 1), :].rearrange("p a n -> p (a n)"), ps_g[u][0:NT, :],
                               ACT.Copy).then_inc(g_hi, 1)
            elif l == 0:
                act.wait_ge(o_done, o0 + t + 3)
                act.activation(o[u][0:NT, :], o[u][0:NT, :], ACT.Relu).then_inc(o_relu, 1)
                act.wait_ge(o_relu, o0 + t + 1)
                act.dma_start(io["h1_dram"][rows_t, 512 * hf:512 * hf + 512], o[u][0:NT, :]).then_inc(o_out[u], 16)
            elif hf == 0:
                act.wait_ge(o_done, o0 + t + 3)
                act.dma_start(io["y_dram"][rows_t, :], o[u][0:NT, :]).then_inc(o_out[u], 16)
            else:
                act.wait_ge(f_var, t + 1)
                act.activation(f_rt[0:NT, :], f_ve[0:NT, :], ACT.Sqrt).then_inc(f_root, 1)
                act.wait_ge(f_norm, t + 1)
                for h, y in enumerate((res[u][0:NT, 1, :], o[u][0:NT, :])):
                    act.activation(rows[u][0:NT, 512 * h:512 * h + 512], y, ACT.Identity, bias=f_sh[u][0:NT, :],
                                   scale=f_rs[u][0:NT, :]).then_inc(f_normed, 1)
                act.wait_ge(f_normed, 2 * t + 2)
                act.dma_start(io["out"][rows_t, :], rows[u][0:NT, :]).then_inc(o_out[u], 16)

        act.wait_ge(bias_in, 32)
        for u in range(2):
            act.sem_inc(o_out[u], 16)
        act.sem_inc(ht_ready, 1)
        for phase in range(len(PHASES)):
            through(act, phase, stage, tile)
        for u in range(2):
            act.wait_ge(o_out[u], 16 * (4 * HF + 1))

    @block.vector
    def _(dve):
        def stage(phase, i, u):
            n0, g0, o0 = counted(phase)
            t = 2 * i + u
            dve.wait_ge(st_hi, n0 + t + 1)
            dve.tensor_tensor(st[u][:, 1, :, :], ht[:, :, bass.ds(t * NT, NT)], raw(st[u][:, 0, :, :]),
                              ALU.subtract).then_inc(st_ready, 1)

        def tile(phase, i, u):
            l, hf, agg = PHASES[phase]
            n0, g0, o0 = counted(phase)
            t = 2 * i + u
            if not agg:
                hi, lo = [g[0:NT, h, bass.ds(t, 1), :].rearrange("p a n -> p (a n)") for h in range(2)]
                dve.wait_ge(g_hi, g0 + t + 1)
                dve.tensor_tensor(lo, ps_g[u][0:NT, :], raw(hi), ALU.subtract).then_inc(g_lo, 1)
                return
            dve.wait_ge(h_used, n0 + t + 3)
            dve.wait_ge(o_out[u], 16 * (HF * (o0 // T) + i) + 16)
            dve.tensor_tensor(o[u][0:NT, :], ps_self[u][0:NT, :], b_rows[0:NT, l, 512 * hf:512 * hf + 512],
                              ALU.add).then_inc(o_biased, 1)
            dve.wait_ge(o_biased, o0 + t + 1)
            if l == 1:
                n = HF * hf + (1 + hf) * i + (1 + hf)
                dve.wait_ge(res_in[u], 16 * n)
                dve.tensor_tensor(o[u][0:NT, :], o[u][0:NT, :], res[u][0:NT, 0, :], ALU.add).then_inc(o_resid, 1)
                dve.wait_ge(o_resid, T * hf + t + 1)
            dve.wait_ge(o_mm, o0 + t + 3)
            dve.scalar_tensor_tensor(out=o[u][0:NT, :], in0=ps_a[u][0:NT, :], scalar=s.deg_inv[0:NT, bass.ds(t, 1)],
                                     in1=o[u][0:NT, :], op0=ALU.mult, op1=ALU.add).then_inc(o_done, 1)
            if l == 1 and hf == 1:
                dve.wait_ge(o_done, o0 + t + 3)
                norm_stats(dve, f_step, 8 * t, f_st[0:NT, :, :], f_mv[0:NT, :], f_ve[0:NT, :], f_var,
                           [res[u][0:NT, 1, :], o[u][0:NT, :]], s.carried)
                dve.wait_ge(f_var, t + 1)
                dve.wait_ge(f_root, t + 1)
                newton_rstd(dve, f_step, 8 * t + 3, f_rs[u][0:NT, :], f_ve[0:NT, :], f_rt[0:NT, :], f_sc[0:NT, :])
                norm_shift(dve, f_sh[u][0:NT, :], f_mv[0:NT, :], f_rs[u][0:NT, :], f_norm)

        dve.sem_inc(g_lo, 2)
        dve.sem_inc(o_done, 2)
        dve.wait_ge(bias_in, 32)
        for phase in range(len(PHASES)):
            through(dve, phase, stage, tile)

    @block.tensor
    def _(pe):
        def turn(l, i, u):
            t = 2 * i + u
            pe.wait_ge(rows_in[u], 16 * (HF * l + i) + 16)
            pe.wait_ge(ht_ready, 2 * (l * T + t) + 1)
            for k in range(KD):
                mm = pe.transpose(ps_t[k // 4][:, (k % 4) * NT:(k % 4 + 1) * NT],
                                  rows[u][0:NT, k * 128:(k + 1) * 128], s.ident[0:NT, 0:NT])
            mm.then_inc(turned, 1)

        def product(out, u, w):
            for k in range(KD):
                for p, (a, b) in enumerate(HALVES):
                    mm = pe.matmul(out, st[u][:, a, k, :], w[:, b, k * 512:(k + 1) * 512],
                                   start=(k == 0 and p == 0), stop=(k == KD - 1 and p == 2))
            return mm

        def tile(phase, i, u):
            l, hf, agg = PHASES[phase]
            n0, g0, o0 = counted(phase)
            t = 2 * i + u
            pe.wait_ge(st_ready, n0 + t + 1)
            if not agg:
                pe.wait_ge(g_lo, g0 + t + 1)
                product(ps_g[u][0:NT, :], u, s.w_neigh).then_inc(h_used, 1)
                return
            pe.wait_ge(o_done, o0 + t + 1)
            product(ps_self[u][0:NT, :], u, s.w_self).then_inc(h_used, 1)
            pe.wait_ge(g_lo, g0 + 2)
            pe.wait_ge(a_in[u], 16 * (HF * (o0 // T) + i) + 16)
            for k in range(T):
                for h in range(2):
                    mm = pe.matmul(ps_a[u][0:NT, :], a_st[u][0:NT, k, :], g[0:NT, h, k, :],
                                   start=(k == 0 and h == 0), stop=(k == T - 1 and h == 1))
            mm.then_inc(o_mm, 1)

        def stage(phase, i, u):
            if phase % 4 == 0:
                turn(phase // 4, i, u)

        pe.sem_inc(h_used, 2)
        pe.sem_inc(o_mm, 2)
        for phase in range(len(PHASES)):
            if phase > 0:
                pe.wait_ge(w_ready, KD * phase)
            through(pe, phase, stage, tile)


class Places:
    pass


def places(nc):
    s = Places()
    at = Map(nc, -(-nc.sbuf_base // 32) * 32)
    s.ident = at("ident", [128, 128], F32)
    s.deg_inv = at("deg_inv", [128, T], F32)
    s.deg = at("deg", [128, T], F32)
    s.ln_gb = at("ln_gb", [128, 2, KD], F32)
    s.biases = at("biases", [128, 4 + 2 + 3 * 2 * LAYERS + 4], F32)
    s.wide_at = at.at
    s.wide = at("wide", [128, 2, KH, NW], F32R)
    s.wide_end = s.at_at = at.at
    s.at_ = at("a_turned", [128, T, NW], F32R)
    s.xn_at = at.at
    s.xn = at("x_norm", [128, 2, KD, NW], F32R)
    s.ring_at = at.at
    s.wring = at("weight_slots", [128, 2, 2, 1024], F32R)
    s.stage_at = at.at
    s.g_at = s.wide_at
    at = Map(nc, s.wide_at + 2 * T * 512 * 4)
    s.w_self = at("w_self", [128, 2, KD * 512], F32R)
    s.w_neigh = at("w_neigh", [128, 2, KD * 512], F32R)
    s.rows = [at(f"h_rows{u}", [128, D], F32) for u in range(2)]
    s.sage_bias = at("sage_bias", [128, 2, D], F32)
    s.late_at = at.at
    s.rows_in = [nc.alloc_semaphore(f"rows_in{u}") for u in range(2)]
    s.bias_in = nc.alloc_semaphore("bias_in")
    s.carried = nc.alloc_semaphore("carried")
    s.banks = [nc.alloc_psum_tensor(f"bank{b}", [128, 512], F32) for b in range(8)]
    return s


def layout(inputs):
    import numpy as np

    a = {name: np.asarray(v) for name, v in inputs.items()}
    g = {name[len("L0_gnn_"):]: v for name, v in a.items() if name.startswith("L0_gnn_")}

    def cols(v):
        return v.reshape(-1, 128).T

    def pair(first, second):
        return np.stack([first, second]).reshape(2, KB, 128, B).transpose(2, 0, 1, 3).reshape(1, 128, 1024)

    empty = np.zeros((B, B), np.float32)
    out = {
        "x": a["x"],
        "src_t": a["src"].reshape(C, EC).T,
        "dst_t": a["dst"].reshape(C, EC).T,
        "pair_weights": np.broadcast_to(np.stack([np.arange(C) // 2 + 1, Q - np.arange(C) // 2])
                                        .astype(np.float32), (EC, 2, C)),
        "iota": np.broadcast_to(np.arange(NW).astype(np.float16), (EC, NW)),
        "ident": np.eye(128, dtype=np.float32),
        "biases": np.concatenate([cols(g["b1"]), cols(g["b2"])] + [cols(g[n]) for n in
                                 ("layer_ba", "layer_ng", "layer_nb")] + [cols(g["bd1"])], 1),
        "bb": g["layer_bb"],
        "w_units": np.concatenate([
            g["W1"].reshape(KD, 128, KH, 128).transpose(2, 1, 0, 3).reshape(KH, 128, 1024),
            g["W2"].reshape(KH, 128, B).transpose(1, 0, 2).reshape(1, 128, 1024),
            pair(g["layer_Wa"][0], empty), pair(g["layer_Wb"][0], g["layer_Wa"][1]),
            g["Wd1"].reshape(KB, 128, H).transpose(1, 0, 2).reshape(1, 128, 1024)]
            + [pair(g["layer_Wb"][i], g["layer_Wa"][i + 1] if i + 1 < LAYERS else empty) for i in range(1, LAYERS)]),
        "Wd2": g["Wd2"],
        "bd2": g["bd2"][None], "out_g": g["out_g"][None], "out_b": g["out_b"][None],
        "w_self": np.stack([a["L1_gnn_W_self0"], a["L1_gnn_W_self1"]]).reshape(2, KD, 128, 2, 512).transpose(0, 3, 1, 2, 4),
        "w_neigh": np.stack([a["L1_gnn_W_neigh0"], a["L1_gnn_W_neigh1"]]).reshape(2, KD, 128, 2, 512).transpose(0, 3, 1, 2, 4),
        "sage_b": np.stack([a["L1_gnn_b0"], a["L1_gnn_b1"]]),
        "ln_gb": np.stack([cols(g["ln_in_g"]), cols(g["ln_in_b"])], 1),
    }
    return {name: np.ascontiguousarray(v) for name, v in out.items()}


def program(nc, io):
    s = places(nc)
    for stage in (graph_block, encoder_block, decoder_block, sage_block):
        with nc.Block() as block:
            stage(nc, block, nc.alloc_semaphore, io, s)


def kernel(**inputs):
    import concourse.bacc as bacc
    import numpy as np
    from concourse.bass_utils import run_bass_kernel_spmd

    nc = bacc.Bacc("TRN2", target_bir_lowering=False, num_devices=1)
    arrays = layout(inputs)
    io = {name: nc.dram_tensor(name, a.shape, mybir.dt.from_np(a.dtype), kind="ExternalInput").ap()
          for name, a in arrays.items()}
    for name, shape in (("at_dram", (T, NT, T, NT)), ("x2_dram", (N, D)), ("h1_dram", (N, D)), ("y_dram", (N, 512))):
        io[name] = nc.dram_tensor(name, shape, F32, kind="Internal").ap()
    io["out"] = nc.dram_tensor("out", (N, D), F32, kind="ExternalOutput").ap()
    program(nc, io)
    r = run_bass_kernel_spmd(nc, [arrays], core_ids=[0])
    return np.asarray(r.results[0]["out"])
```

```python
import concourse.bass as bass
from concourse import mybir

ALU = mybir.AluOpType
ACT = mybir.ActivationFunctionType
AX = mybir.AxisListType
F32 = mybir.dt.float32
F32R = mybir.dt.float32r
BF16 = mybir.dt.bfloat16
F16 = mybir.dt.float16
I32 = mybir.dt.int32

N, E = 1250, 20000
D, H, B, LAYERS = 1024, 512, 256, 3
NT = 125
T = N // NT
EC = 125
C = E // EC
Q = C // 2
KD, KH, KB = D // 128, H // 128, B // 128
CH = 418
NCH = -(-N // CH)
NW = CH * NCH
EPS = 1e-5
HALVES = ((0, 0), (0, 1), (1, 0))
EXACT_COUNTS = 2 ** 12


def raw(ap):
    return ap.bitcast(F32)


class Map:

    def __init__(self, nc, start):
        self.nc, self.at = nc, start

    def __call__(self, name, shape, dt):
        size = 2 if dt in (BF16, F16) else 4
        for n in shape[1:]:
            size *= n
        t = self.nc.alloc_sbuf_tensor_at(name, list(shape), dt, offset=self.at)
        self.at += -(-size // 32) * 32
        return t


def newton_rstd(dve, done, count, rstd, var_eps, root, scratch):
    dve.reciprocal(rstd, root).then_inc(done, 1)
    dve.wait_ge(done, count + 1)
    dve.tensor_tensor(scratch, rstd, rstd, ALU.mult).then_inc(done, 1)
    dve.wait_ge(done, count + 2)
    dve.tensor_tensor(scratch, scratch, var_eps, ALU.mult).then_inc(done, 1)
    dve.wait_ge(done, count + 3)
    dve.tensor_scalar(scratch, scratch, -0.5, 1.5, ALU.mult, ALU.add).then_inc(done, 1)
    dve.wait_ge(done, count + 4)
    dve.tensor_tensor(rstd, rstd, scratch, ALU.mult).then_inc(done, 1)
    dve.wait_ge(done, count + 5)


def carry_waits(eng, carried):
    eng.sem_inc(carried, 1)


def norm_stats(dve, step, count, stats, mean_var, var_eps, var_ready, halves, carried):
    for h, half in enumerate(halves):
        dve.bn_stats(stats[:, h, :], half).then_inc(step, 1)
    dve.wait_ge(step, count + len(halves))
    carry_waits(dve, carried)
    dve.bn_aggr(mean_var, stats).then_inc(step, 1)
    dve.wait_ge(step, count + len(halves) + 1)
    dve.tensor_scalar(var_eps, mean_var[:, 1:2], EPS, None, ALU.add).then_inc(var_ready, 1)


def norm_shift(dve, shift, mean_var, rstd, norm_ready):
    dve.scalar_tensor_tensor(out=shift, in0=mean_var[:, 0:1], scalar=-1.0, in1=rstd,
                             op0=ALU.mult, op1=ALU.mult).then_inc(norm_ready, 1)


def exact_counts(pe, max_degree, products):
    with pe.If(max_degree < EXACT_COUNTS):
        products(lambda ap: ap)
    with pe.Else():
        products(raw)


def graph_block(nc, block, sem, io, s):
    RING = 4
    edges_in, weights_in, consts_in = sem("edges_in"), sem("pair_weights_in"), sem("consts_in")
    x_in = [sem("x_in0"), sem("x_in1")]
    rng_step, range_part, range_cols, range_back, ranges = (sem("rng_step"), sem("range_part"),
        sem("range_cols"), sem("range_back"), sem("ranges"))
    range_col_max = sem("range_col_max")
    hot_ready, hot_free = sem("hot_ready"), sem("hot_free")
    counts_done, counts_out = sem("counts_done"), sem("counts_out")
    var_ready, root_ready, norm_ready, dve_step = (sem("var_ready"), sem("root_ready"),
        sem("norm_ready"), sem("dve_step"))
    xhat_ready, xhat_read, xt_affine, xt_hi, xt_split = (sem("xhat_ready"), sem("xhat_read"),
        sem("xt_affine"), sem("xt_hi"), sem("xt_split"))
    z1_mm, z1_out, z1_turned, z1_relu, z1_hi, z1_split = (sem("z1_mm"), sem("z1_out"), sem("z1_turned"),
        sem("z1_relu"), sem("z1_hi"), sem("z1_split"))
    at_turned, at_out, at_eye = sem("at_turned"), sem("at_out"), sem("at_eye")
    at_stored, at_placed, eye_placed = [[sem(f"{n}{u}") for u in range(2)]
                                        for n in ("at_stored", "at_placed", "eye_placed")]
    w_in, w_hi, w_ready = [sem("gw_in0"), sem("gw_in1")], sem("gw_hi"), sem("gw_ready")
    zeroed, deg_step = sem("zeroed"), sem("deg_step")

    at = Map(nc, s.work_at)
    hot_src = [at(f"hot_src{h}", [128, RING, N], BF16) for h in range(2)]
    hot_dst = [at(f"hot_dst{h}", [128, RING, 128], BF16) for h in range(2)]
    iota = at("iota", [128, NW], F16)
    zeros = at("zeros", [128, 128], BF16)
    counts = [at(f"counts{u}", [128, N], F32) for u in range(2)]
    at_stage1 = at("at_stage1", [128, T, NT], F32)
    w1 = at("w1", [128, 2, KD, H], F32R)
    z1_rows = at("z1_rows", [128, H], F32)
    z1_f32 = at("z1_f32", [128, KH, NT], F32)
    assert at.at <= s.ring_at, at.at - s.ring_at
    xt = nc.alloc_sbuf_tensor_at("xt", [128, 2, KD, NT], F32R, offset=s.ring_at + 8192)
    at = Map(nc, s.work_at)
    src_i, dst_i = at("src_i", [128, C], I32), at("dst_i", [128, C], I32)
    pair_weights = at("pair_weights", [128, 2, C], F32)
    weighted = at("weighted", [128, 2 * T, C], F32)
    at = Map(nc, s.stage_at)
    src_f, dst_f = at("src_f", [128, C], F32), at("dst_f", [128, C], F32)
    part_max = at("part_max", [128, 2 * T], F32)
    col_max = at("col_max", [128, 1], F32)
    row = at("row", [128, 6 * T], F32)
    ranges_i = at("ranges_i", [128, 3 * T], I32)
    x_rows = [at(f"x_rows{u}", [128, D], F32) for u in range(2)]
    xhat = at("xhat", [128, D], F32)
    stats = at("stats", [128, 2, 6], F32)
    mean_var = [at(f"mean_var{u}", [128, 2], F32) for u in range(2)]
    var_eps, root, rstd, shift = [[at(f"{n}{u}", [128, 1], F32) for u in range(2)]
                                  for n in ("var_eps", "root", "rstd", "shift")]
    scratch = at("scratch", [128, 1], F32)
    deg_part = at("deg_part", [128, 3, T], F32)
    xt_f32 = at("xt_f32", [128, KD, NT], F32)
    s.turned_at = at.at
    eye_block = [at(f"eye_block{u}", [128, NT], F32) for u in range(2)]
    at_stage = [at("at_stage0", [128, T, NT], F32), at_stage1]
    assert at.at <= nc.sbuf_usable_end, at.at - nc.sbuf_usable_end
    w_f32 = [b[:, :, :].rearrange("p k n -> p (k n)")[:, 0:1024] for b in at_stage]

    ps_counts, ps_x, ps_a = s.banks[0:3], s.banks[3:5], s.banks[5:8]
    ps_z1, ps_z1_turned = ps_counts[0], ps_x[0]
    COLS = [(0, 418), (418, 834), (834, N)]
    A_GROUPS = [(0, 4), (4, 8), (8, 10)]

    def load_range(eng, t):
        return (eng.value_load(ranges_i[0:1, bass.ds(t, 1)], min_val=0, max_val=Q - 1),
                eng.value_load(ranges_i[0:1, bass.ds(T + t, 1)], min_val=1, max_val=Q),
                eng.value_load(ranges_i[0:1, bass.ds(2 * T + t, 1)], min_val=1, max_val=Q * (T + 1)))

    @block.sync
    def _(sp):
        sp.dma_start(dst_i[0:EC, :], io["dst_t"]).then_inc(edges_in, 16)
        sp.dma_start(src_i[0:EC, :], io["src_t"]).then_inc(edges_in, 16)
        sp.dma_start(pair_weights[0:EC, :, :], io["pair_weights"]).then_inc(weights_in, 16)
        for to, name in ((iota[0:EC, :], "iota"), (s.ident[:, :], "ident"), (s.ln_gb[:, :, :], "ln_gb"),
                         (s.biases[:, :], "biases")):
            sp.dma_start(to, io[name]).then_inc(consts_in, 16)
        for u in range(2):
            sp.dma_start(x_rows[u][0:NT, :], io["x"][u * NT:(u + 1) * NT, :]).then_inc(x_in[u], 16)
        for n in range(KD // 2 + 1):
            if n >= 2:
                sp.wait_ge(w_ready, n - 1)
            unit = io["W1_pairs"][n, :, :] if n < KD // 2 else io["w_units"][0, :, :]
            sp.dma_start(w_f32[n % 2], unit).then_inc(w_in[n % 2], 16)

        def send_turned(i, u):
            t = 2 * i + u
            sp.wait_ge(at_out, 3 * t + 6)
            sp.dma_start(io["at_dram"][bass.ds(t, 1), :, :, :].rearrange("a p k d -> p (a k) d"),
                         at_stage[u][0:NT, :, :]).then_inc(at_stored[u], 16)
            sp.dma_start(raw(s.at_[0:NT, :, bass.ds(t * NT, NT)]), at_stage[u][0:NT, :, :]).then_inc(at_placed[u], 16)

        def send_eye(i, u):
            t = 2 * i + u
            sp.wait_ge(at_placed[u], 16 * i + 32)
            carry_waits(sp, s.carried)
            sp.wait_ge(at_eye, t + 3)
            sp.dma_start(raw(s.at_[0:NT, bass.ds(t, 1), bass.ds(t * NT, NT)]).rearrange("p a n -> p (a n)"),
                         eye_block[u][0:NT, :]).then_inc(eye_placed[u], 16)

        send_turned(0, 0)
        with sp.Fori(0, T // 2 - 1) as i:
            send_turned(i, 1)
            send_eye(i, 0)
            send_turned(i + 1, 0)
            send_eye(i, 1)
        send_turned(T // 2 - 1, 1)
        send_eye(T // 2 - 1, 0)
        s.send_last_eye = lambda: send_eye(T // 2 - 1, 1)
        s.turned_landed = [(landed[u], 16 * (T // 2 + 1)) for landed in (at_stored, eye_placed) for u in range(2)]

    @block.scalar
    def _(act):
        xt_view = [p[:, 0:4 * NT].rearrange("p (k n) -> p k n", k=4) for p in ps_x]
        z1_view = ps_z1_turned[:, 0:KH * NT].rearrange("p (k n) -> p k n", k=KH)
        at_view = [p[0:NT, 0:4 * NT].rearrange("p (k n) -> p k n", k=4) for p in ps_a]

        def take_root(t, u):
            act.wait_ge(var_ready, t + 1)
            act.activation(root[u][0:NT, :], var_eps[u][0:NT, :], ACT.Sqrt).then_inc(root_ready, 1)

        def norm_tile(i, u, last):
            t = 2 * i + u
            act.wait_ge(norm_ready, t + 1)
            act.wait_ge(x_in[u], 16 * i + 16)
            act.wait_ge(xhat_read, t + 1)
            act.activation(xhat[0:NT, :], x_rows[u][0:NT, :], ACT.Identity, bias=shift[u][0:NT, :],
                           scale=rstd[u][0:NT, :]).then_inc(xhat_ready, 1)
            if not last:
                act.wait_ge(xhat_ready, t + 1)
                act.dma_start(x_rows[u][0:NT, :], io["x"][bass.ds((t + 2) * NT, NT), :]).then_inc(x_in[u], 16)

        def read_counts(i, u):
            t = 2 * i + u
            act.wait_ge(counts_done, t + 1)
            for b, (c0, c1) in enumerate(COLS):
                act.activation(counts[u][0:NT, c0:c1], ps_counts[b][0:NT, 0:c1 - c0], ACT.Identity,
                               accum_out=deg_part[0:NT, b, bass.ds(t, 1)]).then_inc(counts_out, 1)

        def affine(i, u):
            t = 2 * i + u
            act.wait_ge(xt_split, t + 1)
            act.wait_ge(xhat_read, t + 2)
            for k in range(KD):
                act.activation(xt_f32[:, k, :], xt_view[k // 4][:, k % 4, :], ACT.Identity,
                               bias=s.ln_gb[:, 1, k:k + 1], scale=s.ln_gb[:, 0, k:k + 1]).then_inc(xt_affine, 1)

        def stage_turned(i, u):
            t = 2 * i + u
            act.wait_ge(at_turned, t + 1)
            act.wait_ge(at_stored[u], 16 * i + 16)
            act.wait_ge(at_placed[u], 16 * i + 16)
            act.wait_ge(at_eye, t + 1)
            for g, (k0, k1) in enumerate(A_GROUPS):
                act.activation(at_stage[u][0:NT, k0:k1, :], at_view[g][:, 0:k1 - k0, :], ACT.Identity)\
                   .then_inc(at_out, 1)

        def z1_to_rows(t):
            act.wait_ge(z1_mm, t + 2)
            act.wait_ge(z1_turned, t + 1)
            act.activation(z1_rows[0:NT, :], ps_z1[0:NT, :], ACT.Identity).then_inc(z1_out, 1)

        def z1_relu_turned(t):
            act.wait_ge(z1_turned, t + 2)
            act.wait_ge(z1_split, t + 1)
            for k in range(KH):
                act.activation(z1_f32[:, k, :], z1_view[:, k, :], ACT.Relu, bias=s.biases[:, k:k + 1])\
                   .then_inc(z1_relu, 1)

        for u in range(2):
            act.sem_inc(at_stored[u], 16)
            act.sem_inc(at_placed[u], 16)
        act.wait_ge(consts_in, 64)
        take_root(0, 0)
        norm_tile(0, 0, False)
        take_root(1, 1)
        read_counts(0, 0)
        norm_tile(0, 1, False)
        take_root(2, 0)
        affine(0, 0)
        act.wait_ge(w_ready, KD // 2 + 1)

        def tile(i, u, load, ahead):
            t = 2 * i + u
            read_counts(i, u)
            norm_tile(i + u, 1 - u, not load)
            if ahead:
                take_root(t + 2, u)
            affine(i, u)
            z1_to_rows(t - 1)
            stage_turned(i + u - 1, 1 - u)
            z1_relu_turned(t - 1)

        tile(0, 1, True, True)
        with act.Fori(1, T // 2 - 2) as i:
            tile(i, 0, True, True)
            tile(i, 1, True, True)
        tile(T // 2 - 2, 0, True, True)
        tile(T // 2 - 2, 1, False, True)
        tile(T // 2 - 1, 0, False, False)
        read_counts(T // 2 - 1, 1)
        affine(T // 2 - 1, 1)
        z1_to_rows(T - 2)
        stage_turned(T // 2 - 1, 0)
        z1_relu_turned(T - 2)
        z1_to_rows(T - 1)
        stage_turned(T // 2 - 1, 1)
        z1_relu_turned(T - 1)

    def split_norm(eng, t):
        eng.wait_ge(xt_affine, KD * (t + 2))
        eng.wait_ge(z1_mm, t + 1)
        carry_waits(eng, s.carried)
        eng.tensor_copy(xt[:, 0, :, :], xt_f32[:, :, :]).then_inc(xt_hi, 1)
        eng.wait_ge(xt_hi, t + 1)
        eng.tensor_tensor(xt[:, 1, :, :], xt_f32[:, :, :], raw(xt[:, 0, :, :]), ALU.subtract).then_inc(xt_split, 1)

    def split_z1(eng, t):
        hi, lo = [s.wide[:, h, :, bass.ds(t * NT, NT)] for h in range(2)]
        eng.wait_ge(z1_relu, KH * (t + 2))
        eng.tensor_copy(hi, z1_f32[:, :, :]).then_inc(z1_hi, 1)
        eng.wait_ge(z1_hi, t + 1)
        eng.tensor_tensor(lo, z1_f32[:, :, :], raw(hi), ALU.subtract).then_inc(z1_split, 1)

    @block.gpsimd
    def _(pool):
        pool.memset(zeros[0:EC, :], 0.0).then_inc(zeroed, 1)
        pool.memset(raw(s.at_[:, :, N:NW]), 0.0).then_inc(zeroed, 1)
        for hl in range(2):
            pool.memset(raw(s.wide[:, hl, :, N:NW]), 0.0).then_inc(zeroed, 1)
        for n in range(KD // 2 + 1):
            hi, lo = [w1[:, h, 2 * n:2 * n + 2, :].rearrange("p k m -> p (k m)") if n < KD // 2
                      else s.wring[:, 0, h, :] for h in range(2)]
            pool.wait_ge(w_in[n % 2], 16 * (n // 2 + 1))
            pool.tensor_copy(hi, w_f32[n % 2]).then_inc(w_hi, 1)
            pool.wait_ge(w_hi, n + 1)
            pool.tensor_tensor(lo, w_f32[n % 2], raw(hi), ALU.subtract).then_inc(w_ready, 1)

        def add_eye(i, u):
            t = 2 * i + u
            pool.wait_ge(at_out, 3 * t + 6)
            pool.wait_ge(eye_placed[u], 16 * i + 16)
            pool.tensor_tensor(eye_block[u][0:NT, :], at_stage[u][0:NT, bass.ds(t, 1), :].rearrange("p a n -> p (a n)"),
                               s.ident[0:NT, 0:NT], ALU.add).then_inc(at_eye, 1)

        pool.sem_inc(xt_split, 1)
        pool.sem_inc(z1_split, 1)
        for u in range(2):
            pool.sem_inc(eye_placed[u], 16)
        pool.sem_inc(at_eye, 2)
        pool.wait_ge(consts_in, 64)
        split_norm(pool, 0)
        with pool.Fori(0, T // 2 - 1) as i:
            for u in range(2):
                split_norm(pool, 2 * i + u + 1)
                add_eye(i, u)
                split_z1(pool, 2 * i + u)
        add_eye(T // 2 - 1, 0)
        split_z1(pool, T - 2)
        add_eye(T // 2 - 1, 1)

    @block.vector
    def _(dve):
        def variance(i, u):
            t = 2 * i + u
            dve.wait_ge(x_in[u], 16 * i + 16)
            norm_stats(dve, dve_step, 8 * t, stats[0:NT, :, :], mean_var[u][0:NT, :], var_eps[u][0:NT, :],
                       var_ready, [x_rows[u][0:NT, 512 * h:512 * h + 512] for h in range(2)], s.carried)

        def normalizer(t, u):
            dve.wait_ge(var_ready, t + 1)
            dve.wait_ge(root_ready, t + 1)
            newton_rstd(dve, dve_step, 8 * t + 3, rstd[u][0:NT, :], var_eps[u][0:NT, :],
                        root[u][0:NT, :], scratch[0:NT, :])
            norm_shift(dve, shift[u][0:NT, :], mean_var[u][0:NT, :], rstd[u][0:NT, :], norm_ready)

        def hot(t):
            first, last, before = load_range(dve, t)
            with dve.Fori(first, last) as q:
                step = q + before
                slot = dve.snap(step & (RING - 1))
                dve.wait_ge(hot_free, step)
                for h in range(2):
                    dve.tensor_scalar(hot_src[h][0:EC, bass.ds(slot, 1), 0:N].rearrange("p a n -> p (a n)"),
                                      iota[0:EC, 0:N], src_f[0:EC, bass.ds(2 * q + h, 1)], None, ALU.is_equal)
                    mask = dve.tensor_scalar(hot_dst[h][0:EC, bass.ds(slot, 1), :].rearrange("p a n -> p (a n)"),
                                      iota[0:EC, bass.ds(t * NT, 128)], dst_f[0:EC, bass.ds(2 * q + h, 1)],
                                      None, ALU.is_equal)
                mask.then_inc(hot_ready, 1)

        dve.wait_ge(edges_in, 32)
        dve.tensor_copy(dst_f[0:EC, :], dst_i[0:EC, :]).then_inc(rng_step, 1)
        dve.tensor_copy(src_f[0:EC, :], src_i[0:EC, :]).then_inc(rng_step, 1)
        dve.wait_ge(rng_step, 2)
        dve.wait_ge(weights_in, 16)
        for t in range(T):
            dve.scalar_tensor_tensor(out=weighted[0:EC, t, :], in0=dst_f[0:EC, :], scalar=float((t + 1) * NT),
                                     in1=pair_weights[0:EC, 0, :], op0=ALU.is_lt, op1=ALU.mult)\
               .then_inc(rng_step, 1)
            dve.scalar_tensor_tensor(out=weighted[0:EC, T + t, :], in0=dst_f[0:EC, :], scalar=float(t * NT),
                                     in1=pair_weights[0:EC, 1, :], op0=ALU.is_ge, op1=ALU.mult)\
               .then_inc(rng_step, 1)
        n = 2 + 2 * T
        dve.wait_ge(rng_step, n)
        dve.tensor_reduce(part_max[0:EC, :], weighted[0:EC, :, :], AX.X, ALU.max).then_inc(range_part, 1)
        variance(0, 0)
        dve.wait_ge(range_cols, 1)
        dve.tensor_reduce(col_max[0:2 * T, :], ps_a[0][0:2 * T, 0:EC], AX.X, ALU.max).then_inc(range_col_max, 1)
        dve.wait_ge(range_back, 1)
        up, down, last, first, width, before = [row[0:1, j * T:(j + 1) * T] for j in range(6)]
        dve.tensor_copy(row[0:1, 0:2 * T], ps_a[1][0:1, 0:2 * T]).then_inc(rng_step, 1)
        dve.wait_ge(rng_step, n + 1)
        dve.tensor_scalar(last, up, 1.0, None, ALU.max).then_inc(rng_step, 1)
        dve.tensor_scalar(first, down, -1.0, float(Q), ALU.mult, ALU.add).then_inc(rng_step, 1)
        dve.wait_ge(rng_step, n + 3)
        dve.scalar_tensor_tensor(out=first, in0=last, scalar=-1.0, in1=first, op0=ALU.add, op1=ALU.min)\
           .then_inc(rng_step, 1)
        dve.wait_ge(rng_step, n + 4)
        dve.tensor_tensor(width, last, first, ALU.subtract).then_inc(rng_step, 1)
        dve.memset(row[0:1, 5 * T:5 * T + 1], 0.0).then_inc(rng_step, 1)
        n += 6
        dve.wait_ge(rng_step, n)
        for t in range(1, T):
            dve.tensor_tensor(before[:, t:t + 1], before[:, t - 1:t], width[:, t - 1:t], ALU.add).then_inc(rng_step, 1)
            n += 1
            dve.wait_ge(rng_step, n)
        dve.tensor_copy(ranges_i[0:1, 0:T], first).then_inc(ranges, 1)
        dve.tensor_copy(ranges_i[0:1, T:2 * T], last).then_inc(ranges, 1)
        dve.scalar_tensor_tensor(out=ranges_i[0:1, 2 * T:3 * T], in0=before, scalar=float(Q), in1=first,
                                 op0=ALU.add, op1=ALU.subtract).then_inc(ranges, 1)
        dve.wait_ge(ranges, 3)
        dve.wait_ge(consts_in, 64)
        with dve.Fori(0, T // 2 - 1) as i:
            for u in range(2):
                normalizer(2 * i + u, u)
                variance(i + u, 1 - u)
                hot(2 * i + u)
        normalizer(T - 2, 0)
        variance(T // 2 - 1, 1)
        hot(T - 2)
        normalizer(T - 1, 1)
        hot(T - 1)
        dve.wait_ge(counts_out, 3 * T)
        dve.tensor_tensor(s.deg[0:NT, :], deg_part[0:NT, 0, :], deg_part[0:NT, 1, :], ALU.add).then_inc(deg_step, 1)
        dve.wait_ge(deg_step, 1)
        dve.tensor_tensor(s.deg[0:NT, :], s.deg[0:NT, :], deg_part[0:NT, 2, :], ALU.add).then_inc(deg_step, 1)
        dve.wait_ge(deg_step, 2)
        dve.tensor_scalar(s.deg[0:NT, :], s.deg[0:NT, :], 1.0, None, ALU.max).then_inc(deg_step, 1)
        dve.wait_ge(deg_step, 3)
        dve.reciprocal(s.deg_inv[0:NT, :], s.deg[0:NT, :]).then_inc(deg_step, 1)
        split_norm(dve, T - 1)
        split_z1(dve, T - 1)

    @block.tensor
    def _(pe):
        pe.wait_ge(consts_in, 64)
        pe.wait_ge(range_part, 1)
        pe.transpose(ps_a[0][0:2 * T, 0:EC], part_max[0:EC, :], s.ident[0:EC, 0:EC]).then_inc(range_cols, 1)
        pe.wait_ge(range_col_max, 1)
        pe.matmul(ps_a[1][0:1, 0:2 * T], col_max[0:2 * T, :], s.ident[0:2 * T, 0:2 * T], start=True, stop=True)\
          .then_inc(range_back, 1)
        pe.sem_inc(hot_free, Q + RING - 1)
        pe.sem_inc(hot_ready, Q - 1)
        pe.sem_inc(xhat_read, 1)
        pe.sem_inc(xt_affine, KD)
        pe.sem_inc(at_out, 3)
        pe.sem_inc(z1_mm, 1)
        pe.sem_inc(z1_turned, 1)
        pe.sem_inc(z1_relu, KH)
        pe.wait_ge(ranges, 3)
        pe.wait_ge(zeroed, 4)

        any_finite = iota.bitcast(BF16)

        def count(t, steps):
            first, last, before = steps
            for b, (c0, c1) in enumerate(COLS):
                pe.matmul(ps_counts[b][:, 0:c1 - c0], zeros[0:EC, :], any_finite[0:EC, 0:c1 - c0],
                          start=True, stop=False)
            with pe.Fori(first, last) as q:
                step = q + before
                slot = pe.snap(step & (RING - 1))
                pe.wait_ge(hot_ready, step)
                for h in range(2):
                    for b, (c0, c1) in enumerate(COLS):
                        mm = pe.matmul(ps_counts[b][:, 0:c1 - c0],
                                       hot_dst[h][0:EC, bass.ds(slot, 1), :].rearrange("p a n -> p (a n)"),
                                       hot_src[h][0:EC, bass.ds(slot, 1), c0:c1].rearrange("p a n -> p (a n)"),
                                       start=False, stop=False)
                mm.then_inc(hot_free, 1)
            for b in range(3):
                mm = pe.matmul(ps_counts[b][:, 0:2], zeros[0:EC, :], any_finite[0:EC, 0:2], start=False, stop=True)
            mm.then_inc(counts_done, 1)

        def turn_norm(t):
            pe.wait_ge(xhat_ready, t + 1)
            pe.wait_ge(xt_affine, KD * (t + 1))
            for k in range(KD):
                mm = pe.transpose(ps_x[k // 4][:, (k % 4) * NT:(k % 4 + 1) * NT],
                                  xhat[0:NT, k * 128:(k + 1) * 128], s.ident[0:NT, 0:NT])
            mm.then_inc(xhat_read, 1)

        def turn_counts(t, u):
            pe.wait_ge(counts_out, 3 * t + 3)
            pe.wait_ge(at_out, 3 * t + 3)
            for g, (k0, k1) in enumerate(A_GROUPS):
                for k in range(k0, k1):
                    mm = pe.transpose(ps_a[g][0:NT, (k - k0) * NT:(k - k0 + 1) * NT],
                                      counts[u][0:NT, k * NT:(k + 1) * NT], s.ident[0:NT, 0:NT])
            mm.then_inc(at_turned, 1)

        def first_dense(t, counts_read):
            pe.wait_ge(xt_split, t + 2)
            pe.wait_ge(counts_out, 3 * counts_read + 1)
            for k in range(KD):
                for p, (a, b) in enumerate(HALVES):
                    mm = pe.matmul(ps_z1[0:NT, :], xt[:, a, k, :], w1[:, b, k, :], start=(k == 0 and p == 0),
                                   stop=(k == KD - 1 and p == 2))
            mm.then_inc(z1_mm, 1)

        def turn_z1(t, norm_read):
            pe.wait_ge(z1_out, t + 1)
            pe.wait_ge(xt_affine, KD * (norm_read + 2))
            for k in range(KH):
                mm = pe.transpose(ps_z1_turned[:, k * NT:(k + 1) * NT], z1_rows[0:NT, k * 128:(k + 1) * 128],
                                  s.ident[0:NT, 0:NT])
            mm.then_inc(z1_turned, 1)

        count(0, load_range(pe, 0))
        turn_norm(0)
        pe.wait_ge(counts_out, 3)
        count(1, load_range(pe, 1))
        turn_norm(1)
        pe.wait_ge(w_ready, KD // 2)
        with pe.Fori(0, T // 2 - 1) as i:
            for u in range(2):
                t = 2 * i + u
                first_dense(t, t + 1)
                steps = load_range(pe, t + 2)
                turn_counts(t, u)
                turn_z1(t, t + 1)
                pe.wait_ge(counts_out, 3 * t + 6)
                count(t + 2, steps)
                pe.wait_ge(z1_relu, KH * (t + 2))
                turn_norm(t + 2)
        first_dense(T - 2, T - 1)
        turn_counts(T - 2, 0)
        turn_z1(T - 2, T - 1)
        first_dense(T - 1, T - 1)
        turn_counts(T - 1, 1)
        pe.wait_ge(z1_relu, KH * T)
        turn_z1(T - 1, T - 1)


def encoder_block(nc, block, sem, io, s):
    w_in, w_hi, w_ready, w_free = sem("w_in"), sem("w_hi"), sem("w_ready"), sem("w_free")
    wd_in = [sem(f"wd_in{k}") for k in range(3)]
    wd_hi, wd_ready = sem("wd_hi"), sem("wd_ready")
    vec_in = sem("vec_in")
    degree_part, degree_row, degree_known = sem("degree_part"), sem("degree_row"), sem("degree_known")
    z_mm, z_out, z_hi, z_split = sem("z_mm"), sem("z_out"), sem("z_hi"), sem("z_split")
    g_mm, g_hi, g_lo = sem("g_mm"), sem("g_hi"), sem("g_lo")
    b_mm, b_added, b_step, b_root, b_norm = (sem("b_mm"), sem("b_added"), sem("b_step"), sem("b_root"),
        sem("b_norm"))
    b_stats, b_var = sem("b_stats"), sem("b_var")
    t_mm, t_out, h_added, h_hi, h_ready = sem("t_mm"), sem("t_out"), sem("h_added"), sem("h_hi"), sem("h_ready")

    at = Map(nc, s.stage_at)
    w_f32 = at("w_f32", [128, 1024], F32)
    act_out = [at(f"act_out{u}", [128, CH], F32) for u in range(2)]
    bb_row = at("bb_row", [128, LAYERS, B], F32)
    b_mv = at("b_mv", [128, T, 2], F32)
    b_ve, b_rt, b_rs, b_scr = [at(f"b_{n}", [128, T], F32) for n in ("ve", "rt", "rs", "scr")]
    b_st = at("b_st", [128, T, 6], F32)
    z_new = [at(f"z_new{u}", [128, KB, NT], F32) for u in range(2)]
    degree_max = at("degree_max", [128, 1], F32)
    assert at.at <= s.turned_at, at.at - s.turned_at
    zb = at("zb", [128, T, B], F32)
    assert at.at <= nc.sbuf_usable_end, at.at - nc.sbuf_usable_end
    at = Map(nc, s.work_at)
    ht = at("ht", [128, 2, KB, NW], F32R)
    zt = at("zt", [128, 2, KB, NW], F32R)
    gn = at("gn", [128, 2, T, B], F32R)
    h_f32 = at("h_f32", [128, KB, NW], F32)
    wd_f32 = [at(f"wd_f32_{u}", [128, D], F32) for u in range(2)] + [w_f32]
    assert at.at <= s.ring_at, at.at - s.ring_at

    ps_z, ps_g, ps_t = s.banks[0:2], s.banks[2:6], s.banks[6:8]

    B2, BA, NG, NB, BD = KH, KH + KB, KH + KB + KB * LAYERS, KH + KB + 2 * KB * LAYERS, KH + KB + 3 * KB * LAYERS
    UNIT_W2, UNIT_WA, UNIT_B0, UNIT_WD1, UNIT_B1 = range(5)
    UNITS = UNIT_B1 + LAYERS - 1
    SLOT = [0, 1, 0, 1, 0]
    FREED = [0, 0, 1, 2, 3]
    ZC = KB * NCH
    TILES = [0] + [min(T, (c + 1) * CH // NT) for c in range(NCH)]
    GROUPS = list(zip(TILES, TILES[1:]))
    ROOTS = len(GROUPS)
    assert GROUPS == [(0, 3), (3, 6), (6, 10)]
    Z0 = ZC
    ZD = Z0 + ZC * LAYERS

    def chunk(j):
        return j % KB, slice((j // KB) * CH, (j // KB + 1) * CH)

    def over_layers(eng, layer):
        with eng.Fori(0, LAYERS - 1) as i:
            layer(i, False)
        layer(LAYERS - 1, True)

    def nodes(t):
        return slice(t * NT, (t + 1) * NT)

    def h_low(eng, i, t):
        eng.wait_ge(h_hi, T * i + t + 1)
        eng.tensor_tensor(ht[:, 1, :, nodes(t)], h_f32[:, :, nodes(t)], raw(ht[:, 0, :, nodes(t)]),
                          ALU.subtract).then_inc(h_ready, 1)

    @block.sync
    def _(sp):
        s.send_last_eye()
        for i in range(LAYERS):
            sp.dma_start(bb_row[0:NT, i, :], io["bb"][i:i + 1, :].to_broadcast([NT, B])).then_inc(vec_in, 16)
        for n in range(1, UNITS):
            if n >= 2:
                sp.wait_ge(w_ready, n)
            sp.dma_start(w_f32[:, :], io["w_units"][n, :, :]).then_inc(w_in, 16)
            if n == UNIT_WD1:
                for k in range(2):
                    sp.dma_start(wd_f32[k][:, :], io["Wd2"][k * 128:(k + 1) * 128, :]).then_inc(wd_in[k], 16)
        sp.wait_ge(w_ready, UNITS)
        sp.dma_start(w_f32[:, :], io["Wd2"][2 * 128:3 * 128, :]).then_inc(wd_in[2], 16)
        sp.wait_ge(wd_ready, 1)
        sp.dma_start(wd_f32[0][:, :], io["Wd2"][3 * 128:4 * 128, :]).then_inc(wd_in[0], 16)

    @block.gpsimd
    def _(pool):
        def halves(n, slot):
            pool.wait_ge(w_in, 16 * (n + 1))
            carry_waits(pool, s.carried)
            pool.tensor_copy(s.wring[:, slot, 0, :], w_f32[:, :]).then_inc(w_hi, 1)
            pool.wait_ge(w_hi, n + 1)
            pool.tensor_tensor(s.wring[:, slot, 1, :], w_f32[:, :], raw(s.wring[:, slot, 0, :]), ALU.subtract)\
                .then_inc(w_ready, 1)

        def layer(i, last):
            def add(t):
                pool.wait_ge(t_out, KB * (T * i + t + 1))
                pool.tensor_tensor(h_f32[:, :, nodes(t)], h_f32[:, :, nodes(t)], z_new[t % 2][:, :, :], ALU.add)\
                    .then_inc(h_added, 1)

            for lo in (0, 3):
                add(lo)
                add(lo + 1)
                h_low(pool, i, lo)
                add(lo + 2)
                h_low(pool, i, lo + 1)
                h_low(pool, i, lo + 2)
            for t in range(6, T):
                add(t)
            if not last:
                pool.wait_ge(w_free, FREED[UNIT_B1] + i)
                halves(UNIT_B1 + i, SLOT[UNIT_B1])

        pool.sem_inc(w_in, 16)
        pool.sem_inc(w_hi, 1)
        pool.sem_inc(w_ready, 1)
        pool.sem_inc(h_added, 2)
        for n in range(1, UNIT_B1):
            if FREED[n]:
                pool.wait_ge(w_free, FREED[n])
            halves(n, SLOT[n])
        over_layers(pool, layer)
        for k in range(KH):
            hi, lo = [s.w_self[:, h, k * D:(k + 1) * D] for h in range(2)]
            pool.wait_ge(wd_hi, k + 1)
            pool.tensor_tensor(lo, wd_f32[k % 3][:, :], raw(hi), ALU.subtract).then_inc(wd_ready, 1)

    @block.scalar
    def _(act):
        def relu(n, j, bias):
            act.wait_ge(z_mm, n + 1)
            act.wait_ge(z_split, n + 1)
            carry_waits(act, s.carried)
            act.activation(act_out[j % 2][:, :], ps_z[j % 2][:, 0:CH], ACT.Relu,
                           bias=s.biases[:, bass.ds(bias, 1)]).then_inc(z_out, 1)

        def g_high(i, t):
            act.wait_ge(g_mm, T * i + t + 1)
            act.activation(gn[0:NT, 0, t, :], ps_g[t % 4][0:NT, 0:B], ACT.Copy).then_inc(g_hi, 1)

        def h_high(i, t):
            act.wait_ge(h_added, T * i + t + 3)
            act.activation(ht[:, 0, :, nodes(t)], h_f32[:, :, nodes(t)], ACT.Copy).then_inc(h_hi, 1)

        def turned(i, t):
            act.wait_ge(t_mm, T * i + t + 1)
            act.wait_ge(h_added, T * i + t + 1)
            carry_waits(act, s.carried)
            for k in range(KB):
                act.activation(z_new[t % 2][:, k, :], ps_t[t % 2][:, k * NT:(k + 1) * NT], ACT.Relu,
                               bias=s.biases[:, bass.ds(NB + KB * i + k, 1)],
                               scale=s.biases[:, bass.ds(NG + KB * i + k, 1)]).then_inc(t_out, 1)

        def roots(i, group):
            lo, hi = GROUPS[group]
            act.wait_ge(b_var, ROOTS * i + group + 1)
            act.activation(b_rt[0:NT, lo:hi], b_ve[0:NT, lo:hi], ACT.Sqrt).then_inc(b_root, 1)

        def wd2_high(k):
            hi = s.w_self[:, 0, k * D:(k + 1) * D]
            act.wait_ge(wd_in[k % 3], 16 * (k // 3 + 1))
            act.activation(hi, wd_f32[k % 3][:, :], ACT.Copy).then_inc(wd_hi, 1)

        def layer(i, last):
            def g(t):
                if not last:
                    g_high(i + 1, t)

            def chunks(lo, hi):
                for j in range(lo, hi):
                    relu(Z0 + ZC * i + j, j, BA + KB * i + j % KB)

            chunks(0, 4)
            roots(i, 0)
            chunks(4, 5)
            turned(i, 0)
            turned(i, 1)
            h_high(i, 0)
            turned(i, 2)
            h_high(i, 1)
            h_high(i, 2)
            roots(i, 1)
            chunks(5, 6)
            turned(i, 3)
            turned(i, 4)
            h_high(i, 3)
            g(0)
            h_high(i, 4)
            g(1)
            turned(i, 5)
            h_high(i, 5)
            roots(i, 2)
            for t in range(2, 6):
                g(t)
            if last:
                for j in range(KH):
                    relu(ZD + j, j, BD + j)
            turned(i, 6)
            for t in range(7, T):
                turned(i, t)
                h_high(i, t - 1)
            g(6)
            h_high(i, T - 1)
            for t in range(7, T):
                g(t)

        for landed, count in s.turned_landed:
            act.wait_ge(landed, count)
        for j in range(ZC):
            act.wait_ge(z_mm, j + 1)
            k, cols = chunk(j)
            act.activation(h_f32[:, k, cols], ps_z[j % 2][:, 0:CH], ACT.Identity,
                           bias=s.biases[:, B2 + k:B2 + k + 1]).then_inc(z_out, 1)
        for t in range(T):
            g_high(0, t)
        over_layers(act, layer)
        for j in range(KH, KH * NCH):
            if j % 2 == 0:
                wd2_high((j - KH) // 2)
            relu(ZD + j, j, BD + j % KH)

    @block.vector
    def _(dve):
        def split(n, dst_hi, dst_lo, src):
            dve.wait_ge(z_out, n + 1)
            dve.tensor_copy(dst_hi, src).then_inc(z_hi, 1)
            dve.wait_ge(z_hi, n + 1)
            dve.tensor_tensor(dst_lo, src, raw(dst_hi), ALU.subtract).then_inc(z_split, 1)

        def g_low(i, t):
            dve.wait_ge(g_hi, T * i + t + 1)
            dve.tensor_tensor(gn[0:NT, 1, t, :], ps_g[t % 4][0:NT, 0:B], raw(gn[0:NT, 0, t, :]),
                              ALU.subtract).then_inc(g_lo, 1)

        def add_bias(i, t):
            dve.wait_ge(b_mm, T * i + t + 1)
            dve.tensor_tensor(zb[0:NT, t, :], ps_g[2 + t % 2][0:NT, 0:B],
                              bb_row[0:NT, bass.ds(i, 1), :].rearrange("p a n -> p (a n)"), ALU.add)\
               .then_inc(b_added, 1)
            dve.wait_ge(b_added, T * i + t + 1)
            dve.bn_stats(b_st[0:NT, t, :], zb[0:NT, t, :]).then_inc(b_stats, 1)

        def variances(i, group):
            lo, hi = GROUPS[group]
            dve.wait_ge(b_stats, T * i + hi)
            carry_waits(dve, s.carried)
            for t in range(lo, hi):
                dve.bn_aggr(b_mv[0:NT, t, :], b_st[0:NT, t, :]).then_inc(b_step, 1)
            dve.wait_ge(b_step, (T + 5 * ROOTS) * i + hi + 5 * group)
            dve.tensor_scalar(b_ve[0:NT, lo:hi], b_mv[0:NT, lo:hi, 1], EPS, None, ALU.add).then_inc(b_var, 1)

        def normalize(i, group):
            lo, hi = GROUPS[group]
            dve.wait_ge(b_var, ROOTS * i + group + 1)
            dve.wait_ge(b_root, ROOTS * i + group + 1)
            newton_rstd(dve, b_step, (T + 5 * ROOTS) * i + hi + 5 * group, b_rs[0:NT, lo:hi], b_ve[0:NT, lo:hi],
                        b_rt[0:NT, lo:hi], b_scr[0:NT, lo:hi])
            for t in range(lo, hi):
                dve.tensor_scalar(zb[0:NT, t, :], zb[0:NT, t, :], b_mv[0:NT, t, 0:1], b_rs[0:NT, t:t + 1],
                                  ALU.subtract, ALU.mult).then_inc(b_norm, 1)

        def layer(i, last):
            def chunks(lo, hi):
                for j in range(lo, hi):
                    k, cols = chunk(j)
                    split(Z0 + ZC * i + j, zt[:, 0, k, cols], zt[:, 1, k, cols], act_out[j % 2][:, :])

            def g(t):
                if not last:
                    g_low(i + 1, t)

            chunks(0, 3)
            for t in range(0, 3):
                add_bias(i, t)
            chunks(3, 4)
            variances(i, 0)
            normalize(i, 0)
            chunks(4, 5)
            for t in range(3, 6):
                add_bias(i, t)
            variances(i, 1)
            normalize(i, 1)
            chunks(5, 6)
            add_bias(i, 6)
            g(0)
            add_bias(i, 7)
            add_bias(i, 8)
            g(1)
            add_bias(i, 9)
            variances(i, 2)
            normalize(i, 2)
            for t in range(2, 6):
                g(t)
            if last:
                for j in range(KH):
                    split_wide(j)
            for t in range(6, T - 1):
                h_low(dve, i, t)
            g(6)
            h_low(dve, i, T - 1)
            for t in range(7, T):
                g(t)

        def split_wide(j):
            k, c = j % KH, j // KH
            hi, lo = [s.wide[:, hl, k, c * CH:(c + 1) * CH] for hl in range(2)]
            split(ZD + j, hi, lo, act_out[j % 2][:, :])

        dve.tensor_reduce(degree_max[0:NT, :], s.deg[0:NT, :], AX.X, ALU.max).then_inc(degree_part, 1)
        dve.sem_inc(z_split, 2)
        dve.wait_ge(vec_in, 16 * LAYERS)
        for landed, count in s.turned_landed:
            dve.wait_ge(landed, count)
        dve.wait_ge(degree_row, 1)
        dve.tensor_reduce(s.max_degree[0:1, :], ps_t[0][0:1, 0:NT], AX.X, ALU.max).then_inc(degree_known, 1)
        for j in range(ZC):
            k, cols = chunk(j)
            split(j, ht[:, 0, k, cols], ht[:, 1, k, cols], h_f32[:, k, cols])
        for t in range(T):
            g_low(0, t)
        over_layers(dve, layer)
        for j in range(KH, KH * NCH):
            split_wide(j)

    @block.tensor
    def _(pe):
        def dense(out, w, x, k_tiles):
            for k in range(k_tiles):
                for p, (a, b) in enumerate(HALVES):
                    mm = pe.matmul(out, w(a, k), x(b, k), start=(k == 0 and p == 0),
                                   stop=(k == k_tiles - 1 and p == 2))
            return mm

        def weights(slot, half):
            return lambda h, k: s.wring[:, slot, h, (half * KB + k) * B:(half * KB + k + 1) * B]

        def g_tile(t, w):
            dense(ps_g[t % 4][0:NT, 0:B], lambda h, k: ht[:, h, k, nodes(t)], w, KB).then_inc(g_mm, 1)

        def next_g(i, lo, hi):
            for t in range(lo, hi):
                pe.wait_ge(h_ready, T * i + t + 1)
                if 2 <= t < 4:
                    pe.wait_ge(b_added, T * i + T)
                if t >= 4:
                    pe.wait_ge(g_lo, T * (i + 1) + t - 3)
                g_tile(t, weights(SLOT[UNIT_B0], 1))

        def with_counts(i, j):
            m, cols = chunk(j)
            pe.wait_ge(z_split, Z0 + ZC * i + j + 1)

            def products(cast):
                for k in range(T):
                    if j == 0:
                        pe.wait_ge(g_lo, T * i + k + 1)
                    for h in range(2):
                        mm = pe.matmul(ps_z[j % 2][:, 0:CH], cast(gn[0:NT, h, k, m * 128:(m + 1) * 128]),
                                       cast(s.at_[0:NT, k, cols]), start=(k == 0 and h == 0),
                                       stop=(k == T - 1 and h == 1))
                mm.then_inc(z_mm, 1)

            exact_counts(pe, max_degree, products)

        def second(i, c):
            if c == 0:
                pe.wait_ge(w_ready, UNIT_B1 + i)
            pe.wait_ge(z_split, Z0 + ZC * i + KB * (c + 1) + 2)
            for t in range(TILES[c], TILES[c + 1]):
                if t >= 2:
                    pe.wait_ge(b_added, T * i + t - 1)
                mm = dense(ps_g[2 + t % 2][0:NT, 0:B], lambda h, k: zt[:, h, k, nodes(t)],
                           weights(SLOT[UNIT_B0], 0), KB)
                mm.then_inc(b_mm, 1)

        def turn(i, lo, hi):
            for t in range(lo, hi):
                pe.wait_ge(b_norm, T * i + t + 1)
                if t >= 2:
                    pe.wait_ge(t_out, KB * (T * i + t - 1))
                for k in range(KB):
                    mm = pe.transpose(ps_t[t % 2][:, k * NT:(k + 1) * NT], zb[0:NT, t, k * 128:(k + 1) * 128],
                                      s.ident[0:NT, 0:NT])
                mm.then_inc(t_mm, 1)

        def last_dense(c):
            wd1 = s.wring[:, SLOT[UNIT_WD1], :, :].rearrange("p h (k m) -> p h k m", k=KB)
            cols = slice(c * CH, (c + 1) * CH)
            pe.wait_ge(h_ready, T * (LAYERS - 1) + min(T, -(-(c + 1) * CH // NT)))
            for m in range(KH):
                j = KH * c + m
                pe.wait_ge(z_split, ZD + j + 1)
                mm = dense(ps_z[j % 2][:, 0:CH], lambda h, k: wd1[:, h, k, m * 128:(m + 1) * 128],
                           lambda h, k: ht[:, h, k, cols], KB)
                mm.then_inc(z_mm, 1)

        def layer(i, last):
            for j in range(3):
                with_counts(i, j)
            second(i, 0)
            with_counts(i, 3)
            with_counts(i, 4)
            turn(i, 0, 2)
            second(i, 1)
            turn(i, 2, 3)
            with_counts(i, 5)
            turn(i, 3, 5)
            if not last:
                next_g(i, 0, 2)
            second(i, 2)
            turn(i, 5, 6)
            if last:
                last_dense(0)
                turn(i, 6, T)
                for c in range(1, NCH):
                    last_dense(c)
                return
            next_g(i, 2, 6)
            turn(i, 6, T)
            next_g(i, 6, T)
            pe.wait_ge(g_mm, T * i + 2 * T)
            pe.sem_inc(w_free, 1)

        pe.wait_ge(degree_part, 1)
        pe.transpose(ps_t[0][0:1, 0:NT], degree_max[0:NT, :], s.ident[0:NT, 0:NT]).then_inc(degree_row, 1)
        w2 = s.wring[:, 0, :, :].rearrange("p h (k m) -> p h k m", k=KH)
        pe.wait_ge(w_ready, UNIT_W2 + 1)
        for j in range(ZC):
            m, cols = chunk(j)
            if j >= 2:
                pe.wait_ge(z_out, j - 1)
            mm = dense(ps_z[j % 2][:, 0:CH], lambda h, k: w2[:, h, k, m * 128:(m + 1) * 128],
                       lambda h, k: s.wide[:, h, k, cols], KH)
            mm.then_inc(z_mm, 1)
        pe.wait_ge(z_mm, ZC)
        pe.sem_inc(w_free, 1)
        pe.wait_ge(w_ready, UNIT_WA + 1)
        for t in range(T):
            pe.wait_ge(z_split, 2 + KB * (((t + 1) * NT - 1) // CH + 1))
            if t >= 4:
                pe.wait_ge(g_lo, t - 3)
            g_tile(t, weights(SLOT[UNIT_WA], 0))
        pe.wait_ge(g_mm, T)
        pe.sem_inc(w_free, 1)
        for landed, count in s.turned_landed:
            pe.wait_ge(landed, count)
        pe.wait_ge(degree_known, 1)
        max_degree = pe.value_load(s.max_degree[0:1, 0:1], min_val=0, max_val=E)
        over_layers(pe, layer)


def decoder_block(nc, block, sem, io, s):
    x_in = [sem("dx_in0"), sem("dx_in1")]
    bd_in, row_in, bias_split, bias_hi, const_set = sem("bd_in"), sem("row_in"), sem("bias_split"), sem("bias_hi"), sem("const_set")
    y_mm, y_added, xo_ready, z1_ready, z2_ready = (sem("y_mm"), sem("y_added"), sem("xo_ready"),
        sem("z1_ready"), sem("z2_ready"))
    mean_ready, sq_ready, root_ready, rstd_step, rstd_ready = [[sem(f"dec_{n}{j}") for j in range(2)]
        for n in ("mean_ready", "sq_ready", "root_ready", "rstd_step", "rstd_ready")]
    shift_ready, x2_ready = sem("shift_ready"), sem("x2_ready")
    x2_out = [sem("x2_out0"), sem("x2_out1")]
    wn_in, wn_hi, wn_ready = [sem("wn_in0"), sem("wn_in1")], sem("wn_hi"), sem("wn_ready")

    at = Map(nc, s.late_at)
    gain_row, bias_row = at("gain_row", [128, D], F32), at("bias_row", [128, D], F32)
    bd_f32 = at("bd_f32", [128, D], F32)
    bd = at("bd", [128, 2, D], F32R)
    ones = at("ones", [128, 128], F32R)
    ones_f32 = at("ones_f32", [128, 128], F32)
    eps = at("eps", [128, 1], F32)
    xr, xo, y, z = [[at(f"{n}{u}", [128, D], F32) for u in range(2)]
                    for n in ("dec_x", "dec_xo", "dec_y", "dec_z")]
    squares = at("squares", [128, D], F32)
    y_sum = [at(f"y_sum{u}", [128, 2], F32) for u in range(2)]
    z_sum = [at(f"z_sum{u}", [128, 1], F32) for u in range(2)]
    minus_mean, square_sum, var_eps, root, rstd, scratch = [
        [[at(f"dec_{n}{j}{u}", [128, 1], F32) for u in range(2)] for j in range(2)]
        for n in ("minus_mean", "square_sum", "var_eps", "root", "rstd", "scratch")]
    shift = [at(f"dec_shift{u}", [128, 1], F32) for u in range(2)]
    w_f32 = [at(f"wn_f32_{u}", [128, 512], F32) for u in range(2)]
    end = nc.sbuf_usable_end - nc.sbuf_usable_end % 32 - 2 * 4 * D
    assert at.at <= end, at.at - end
    at = Map(nc, end)
    x2 = [at(f"dec_x2{u}", [128, D], F32) for u in range(2)]
    banks = s.banks

    def by_pairs(eng, tile):
        tile(0, 0, True)
        tile(0, 1, False)
        with eng.Fori(1, T // 2) as i:
            for u in range(2):
                tile(i, u, False)

    def before(i, u):
        return (i, 0) if u else (i - 1, 1)

    @block.sync
    def _(sp):
        sp.dma_start(bd_f32[0:1, :], io["bd2"]).then_inc(bd_in, 16)
        for u in range(2):
            sp.dma_start(xr[u][0:NT, :], io["x"][u * NT:(u + 1) * NT, :]).then_inc(x_in[u], 16)
        sp.dma_start(gain_row[0:NT, :], io["out_g"].to_broadcast([NT, D])).then_inc(row_in, 16)
        sp.dma_start(bias_row[0:NT, :], io["out_b"].to_broadcast([NT, D])).then_inc(row_in, 16)

        def store(i, u):
            t = 2 * i + u
            sp.wait_ge(x2_ready, t + 3)
            sp.dma_start(io["x2_dram"][bass.ds(t * NT, NT), :], x2[u][0:NT, :]).then_inc(x2_out[u], 16)

        with sp.Fori(0, T // 2 - 1) as i:
            for u in range(2):
                t = 2 * i + u
                sp.wait_ge(xo_ready, t + 1)
                sp.wait_ge(y_added, 2 * t + 2)
                sp.dma_start(xr[u][0:NT, :], io["x"][bass.ds((t + 2) * NT, NT), :]).then_inc(x_in[u], 16)
                store(i, u)
        for layer in range(2):
            sp.dma_start(s.sage_bias[0:NT, layer, :], io["sage_b"][layer:layer + 1, :].to_broadcast([NT, D]))\
              .then_inc(s.bias_in, 16)
        for u in range(2):
            sp.wait_ge(x2_out[u], 48)
            sp.dma_start(s.rows[u][0:NT, :], io["x2_dram"][u * NT:(u + 1) * NT, :]).then_inc(s.rows_in[u], 16)
        for u in range(2):
            store(T // 2 - 1, u)
        s.x2_landed = [(x2_out[u], 16 * (T // 2 + 1)) for u in range(2)]

    @block.gpsimd
    def _(pool):
        pool.memset(ones_f32[:, :], 1.0).then_inc(const_set, 1)
        pool.memset(eps[:, :], EPS).then_inc(const_set, 1)
        pool.wait_ge(const_set, 2)
        pool.tensor_copy(ones[:, :], ones_f32[:, :]).then_inc(const_set, 1)
        for u in range(2):
            pool.dma_start(w_f32[u][:, :], io["w_neigh"][0, 0, u]).then_inc(wn_in[u], 16)
        pool.wait_ge(row_in, 32)
        for t in range(T):
            i, u = divmod(t, 2)
            pool.wait_ge(x_in[u], 16 * i + 16)
            if t >= 2:
                pool.wait_ge(z2_ready, t - 1)
            pool.tensor_tensor(xo[u][0:NT, :], xr[u][0:NT, :], bias_row[0:NT, :], ALU.add).then_inc(xo_ready, 1)
            if t < KD:
                pool.wait_ge(wn_in[u], 16 * i + 16)
                hi, lo = [s.w_neigh[:, h, t * 512:(t + 1) * 512] for h in range(2)]
                pool.tensor_copy(hi, w_f32[u][:, :]).then_inc(wn_hi, 1)
                pool.wait_ge(wn_hi, t + 1)
                pool.tensor_tensor(lo, w_f32[u][:, :], raw(hi), ALU.subtract).then_inc(wn_ready, 1)
                if t + 2 < KD:
                    pool.wait_ge(wn_ready, t + 1)
                    pool.dma_start(w_f32[u][:, :], io["w_neigh"][0, 0, t + 2]).then_inc(wn_in[u], 16)

    @block.scalar
    def _(act):
        def deviations(i, u, j):
            t = 2 * i + u
            act.wait_ge(mean_ready[j], t + 1)
            act.activation(squares[0:NT, :], (z if j else y)[u][0:NT, :], ACT.Square,
                           bias=minus_mean[j][u][0:NT, :], accum_out=square_sum[j][u][0:NT, :]).then_inc(sq_ready[j], 1)
            act.wait_ge(sq_ready[j], t + 1)
            act.activation(root[j][u][0:NT, :], square_sum[j][u][0:NT, :], ACT.Sqrt, bias=eps[0:NT, :],
                           scale=1.0 / D).then_inc(root_ready[j], 1)

        def normalize(i, u):
            act.wait_ge(shift_ready, 2 * i + u + 1)
            act.wait_ge(x2_out[u], 16 * i + 16)
            act.activation(x2[u][0:NT, :], z[u][0:NT, :], ACT.Identity, bias=shift[u][0:NT, :],
                           scale=rstd[1][u][0:NT, :]).then_inc(x2_ready, 1)

        def tile(i, u, first):
            deviations(i, u, 0)
            if not first:
                normalize(*before(i, u))
            deviations(i, u, 1)

        for u in range(2):
            act.sem_inc(x2_out[u], 16)
        act.wait_ge(const_set, 2)
        by_pairs(act, tile)
        normalize(T // 2 - 1, 1)

    @block.vector
    def _(dve):
        def rstds(i, u, j):
            t = 2 * i + u
            ve, rs, sc = var_eps[j][u][0:NT, :], rstd[j][u][0:NT, :], scratch[j][u][0:NT, :]
            dve.wait_ge(sq_ready[j], t + 1)
            dve.tensor_scalar(ve, square_sum[j][u][0:NT, :], 1.0 / D, EPS, ALU.mult, ALU.add).then_inc(rstd_step[j], 1)
            dve.wait_ge(root_ready[j], t + 1)
            dve.reciprocal(rs, root[j][u][0:NT, :]).then_inc(rstd_step[j], 1)
            dve.wait_ge(rstd_step[j], 4 * t + 2)
            dve.scalar_tensor_tensor(out=sc, in0=rs, scalar=ve, in1=rs, op0=ALU.mult, op1=ALU.mult)\
               .then_inc(rstd_step[j], 1)
            dve.wait_ge(rstd_step[j], 4 * t + 3)
            dve.tensor_scalar(sc, sc, -0.5, 1.5, ALU.mult, ALU.add).then_inc(rstd_step[j], 1)
            dve.wait_ge(rstd_step[j], 4 * t + 4)
            dve.tensor_tensor(rs, rs, sc, ALU.mult).then_inc(rstd_ready[j], 1)
            dve.wait_ge(rstd_ready[j], t + 1)

        def second_rstd(i, u):
            rstds(i, u, 1)
            dve.tensor_tensor(shift[u][0:NT, :], minus_mean[1][u][0:NT, :], rstd[1][u][0:NT, :], ALU.mult)\
               .then_inc(shift_ready, 1)

        def tile(i, u, first):
            t = 2 * i + u
            dve.wait_ge(y_mm, t + 1)
            dve.wait_ge(x_in[u], 16 * i + 16)
            for c in range(2):
                cols = slice(512 * c, 512 * c + 512)
                dve.scalar_tensor_tensor(out=y[u][0:NT, cols], in0=banks[2 * u + c][0:NT, :], scalar=1.0,
                                         in1=xr[u][0:NT, cols], op0=ALU.mult, op1=ALU.add,
                                         accum_out=y_sum[u][0:NT, c:c + 1]).then_inc(y_added, 1)
            dve.wait_ge(y_added, 2 * t + 2)
            dve.tensor_scalar(minus_mean[0][u][0:NT, :], y_sum[u][0:NT, 0:1], y_sum[u][0:NT, 1:2], -1.0 / D,
                              ALU.add, ALU.mult).then_inc(mean_ready[0], 1)
            if not first:
                second_rstd(*before(i, u))
            dve.wait_ge(mean_ready[0], t + 1)
            dve.wait_ge(x2_ready, t + 1)
            dve.scalar_tensor_tensor(out=z[u][0:NT, :], in0=y[u][0:NT, :], scalar=minus_mean[0][u][0:NT, :],
                                     in1=gain_row[0:NT, :], op0=ALU.add, op1=ALU.mult).then_inc(z1_ready, 1)
            rstds(i, u, 0)
            dve.wait_ge(z1_ready, t + 1)
            dve.wait_ge(xo_ready, t + 1)
            dve.scalar_tensor_tensor(out=z[u][0:NT, :], in0=z[u][0:NT, :], scalar=rstd[0][u][0:NT, :],
                                     in1=xo[u][0:NT, :], op0=ALU.mult, op1=ALU.add,
                                     accum_out=z_sum[u][0:NT, :]).then_inc(z2_ready, 1)
            dve.wait_ge(z2_ready, t + 1)
            dve.tensor_scalar(minus_mean[1][u][0:NT, :], z_sum[u][0:NT, :], -1.0 / D, None, ALU.mult)\
               .then_inc(mean_ready[1], 1)

        dve.sem_inc(x2_ready, 2)
        dve.wait_ge(bd_in, 16)
        dve.tensor_copy(bd[0:1, 0, :], bd_f32[0:1, :]).then_inc(bias_hi, 1)
        dve.wait_ge(bias_hi, 1)
        dve.tensor_tensor(bd[0:1, 1, :], bd_f32[0:1, :], raw(bd[0:1, 0, :]), ALU.subtract).then_inc(bias_split, 1)
        dve.wait_ge(row_in, 32)
        by_pairs(dve, tile)
        second_rstd(T // 2 - 1, 1)

    @block.tensor
    def _(pe):
        for t in range(T):
            if t >= 2:
                pe.wait_ge(y_added, 2 * (t - 1))
            outs = [banks[2 * (t % 2) + c][0:NT, :] for c in range(2)]
            for c, out in enumerate(outs):
                for k in range(KH):
                    for p, (a, b) in enumerate(HALVES):
                        pe.matmul(out, s.wide[:, a, k, t * NT:(t + 1) * NT],
                                  s.w_self[:, b, k * D + 512 * c:k * D + 512 * c + 512],
                                  start=(k == 0 and p == 0), stop=False)
            if t == 0:
                pe.wait_ge(bias_split, 1)
                pe.wait_ge(const_set, 3)
            for c, out in enumerate(outs):
                for h in range(2):
                    mm = pe.matmul(out, ones[0:1, 0:NT], bd[0:1, h, 512 * c:512 * c + 512],
                                   start=False, stop=(h == 1))
            mm.then_inc(y_mm, 1)
        pe.wait_ge(s.rows_in[0], 16)
        turn_rows(pe, s, 0)


def turn_rows(pe, s, u):
    for k in range(KD):
        mm = pe.transpose(s.banks[4 + k // 4][:, (k % 4) * NT:(k % 4 + 1) * NT],
                          s.rows[u][0:NT, k * 128:(k + 1) * 128], s.ident[0:NT, 0:NT])
    mm.then_inc(s.turned, 1)


def sage_block(nc, block, sem, io, s):
    rows_in, bias_in, rows, b_rows = s.rows_in, s.bias_in, s.rows, s.sage_bias
    turned, ht_ready, st_hi, st_ready, h_used = (s.turned, sem("ht_ready"), sem("st_hi"),
        sem("st_ready"), sem("h_used"))
    g_hi, g_lo = sem("sg_hi"), sem("sg_lo")
    a_in = [sem("a_in0"), sem("a_in1")]
    o_mm, o_biased, o_resid, o_done, o_relu = (sem("o_mm"), sem("o_biased"), sem("o_resid"),
        sem("o_done"), sem("o_relu"))
    o_out = [sem("o_out0"), sem("o_out1")]
    res_in = [sem("res_in0"), sem("res_in1")]
    w_in, w_hi, w_ready = [sem("sw_in0"), sem("sw_in1")], sem("sw_hi"), sem("sw_ready")
    f_step, f_var, f_root, f_norm, f_normed = sem("f_step"), sem("f_var"), sem("f_root"), sem("f_norm"), sem("f_normed")

    g = nc.alloc_sbuf_tensor_at("g_rows", [128, 2, T, 512], F32R, offset=s.g_at)
    at = Map(nc, s.late_at)
    ht = at("h_turned", [128, KD, N], F32)
    st = [at(f"h_stage{u}", [128, 2, KD, NT], F32R) for u in range(2)]
    a_st = [at(f"a_stage{u}", [128, T, NT], F32R) for u in range(2)]
    w_f32 = [at(f"w_stage{u}", [128, 512], F32) for u in range(2)]
    o = [at(f"o{u}", [128, 512], F32) for u in range(2)]
    res = [at(f"res{u}", [128, 2, 512], F32) for u in range(2)]
    f_st = at("f_st", [128, 2, 6], F32)
    f_mv = at("f_mv", [128, 2], F32)
    f_ve, f_rt, f_sc = [at(f"f_{n}", [128, 1], F32) for n in ("ve", "rt", "sc")]
    f_rs, f_sh = [[at(f"f_{n}{u}", [128, 1], F32) for u in range(2)] for n in ("rs", "sh")]
    assert at.at <= nc.sbuf_usable_end, at.at
    ps_g, ps_self, ps_t, ps_a = s.banks[0:2], s.banks[2:4], s.banks[4:6], s.banks[6:8]
    HF = T // 2
    PHASES = [(l, hf, agg) for l in range(2) for hf in range(2) for agg in range(2)]

    def counted(phase):
        return T * phase, T * ((phase + 1) // 2), T * (phase // 2)

    @block.sync
    def _(sp):
        for landed, count in s.x2_landed:
            sp.wait_ge(landed, count)

        def load_rows(l, i, u):
            if l == 1:
                sp.wait_ge(o_out[u], 16 * (HF + 2) + 16 * i)
            sp.dma_start(rows[u][0:NT, :], io["h1_dram" if l else "x2_dram"][bass.ds((2 * i + u) * NT, NT), :])\
              .then_inc(rows_in[u], 16)

        def load_counts(phase, i, u):
            l, hf, agg = PHASES[phase]
            o0 = counted(phase)[2]
            t = 2 * i + u
            sp.wait_ge(o_mm, o0 + t + 1)
            sp.dma_start(raw(a_st[u][0:NT, :, :]),
                         io["at_dram"][bass.ds(t, 1), :, :, :].rearrange("a p k d -> p (a k) d")).then_inc(a_in[u], 16)
            if l == 1:
                if hf == 0:
                    sp.wait_ge(o_out[u], 16 * (T + 1) + 16 * i)
                else:
                    sp.wait_ge(o_out[u], 16 * (T + 1) + 16 * HF)
                    sp.wait_ge(f_normed, 2 * t + 2)
                sp.dma_start(res[u][0:NT, 0, :], io["x2_dram"][bass.ds(t * NT, NT), 512 * hf:512 * hf + 512])\
                  .then_inc(res_in[u], 16)
                if hf == 1:
                    sp.dma_start(res[u][0:NT, 1, :], io["y_dram"][bass.ds(t * NT, NT), :]).then_inc(res_in[u], 16)

        for phase, (l, hf, agg) in enumerate(PHASES):
            if phase % 4 == 0:
                with sp.Fori(1, HF) as i:
                    for u in range(2):
                        sp.wait_ge(turned, l * T + 2 * i + u - 1)
                        load_rows(l, i, u)
            if agg:
                with sp.Fori(0, HF - 1) as i:
                    for u in range(2):
                        load_counts(phase, i, u)
                if phase == 3:
                    for u in range(2):
                        load_rows(1, 0, u)
                for u in range(2):
                    load_counts(phase, HF - 1, u)

    @block.gpsimd
    def _(pool):
        for phase, (l, hf, agg) in enumerate(PHASES):
            if phase == 0:
                continue
            w = io["w_self" if agg else "w_neigh"]
            to = s.w_self if agg else s.w_neigh
            for u in range(2):
                pool.dma_start(w_f32[u][:, :], w[l, hf, u]).then_inc(w_in[u], 16)
            if phase >= 2:
                pool.wait_ge(h_used, T * (phase - 1) + 2)
            for k in range(KD):
                u = k % 2
                c = KD * (phase - 1) + k
                hi, lo = [to[:, h, k * 512:(k + 1) * 512] for h in range(2)]
                pool.wait_ge(w_in[u], 16 * (c // 2 + 1))
                pool.tensor_copy(hi, w_f32[u][:, :]).then_inc(w_hi, 1)
                pool.wait_ge(w_hi, c + 1)
                pool.tensor_tensor(lo, w_f32[u][:, :], raw(hi), ALU.subtract).then_inc(w_ready, 1)
                pool.wait_ge(w_ready, c + 1)
                if k + 2 < KD:
                    pool.dma_start(w_f32[u][:, :], w[l, hf, k + 2]).then_inc(w_in[u], 16)

    def through(eng, phase, stage, tile):
        if phase == 0:
            for u in range(2):
                stage(phase, 0, u)
        with eng.Fori(0, HF - 1) as i:
            for u in range(2):
                stage(phase, i + 1, u)
                tile(phase, i, u)
        for u in range(2):
            if phase + 1 < len(PHASES):
                stage(phase + 1, 0, u)
            tile(phase, HF - 1, u)

    @block.scalar
    def _(act):
        def stage(phase, i, u):
            n0, g0, o0 = counted(phase)
            t = 2 * i + u
            cols = bass.ds(t * NT, NT)
            if phase % 4 == 0:
                l = phase // 4
                act.wait_ge(turned, l * T + t + 1)
                carry_waits(act, s.carried)
                for b in range(2):
                    act.activation(ht[:, 4 * b:4 * b + 4, cols],
                                   ps_t[b][:, 0:4 * NT].rearrange("p (k n) -> p k n", k=4), ACT.Copy)\
                       .then_inc(ht_ready, 1)
                act.wait_ge(ht_ready, 2 * (l * T + t) + 3)
            act.wait_ge(h_used, n0 + t + 1)
            carry_waits(act, s.carried)
            act.activation(st[u][:, 0, :, :], ht[:, :, cols], ACT.Copy).then_inc(st_hi, 1)

        def tile(phase, i, u):
            l, hf, agg = PHASES[phase]
            n0, g0, o0 = counted(phase)
            t = 2 * i + u
            rows_t = bass.ds(t * NT, NT)
            if not agg:
                act.wait_ge(h_used, n0 + t + 3)
                carry_waits(act, s.carried)
                act.activation(g[0:NT, 0, bass.ds(t, 1), :].rearrange("p a n -> p (a n)"), ps_g[u][0:NT, :],
                               ACT.Copy).then_inc(g_hi, 1)
            elif l == 0:
                act.wait_ge(o_done, o0 + t + 3)
                act.activation(o[u][0:NT, :], o[u][0:NT, :], ACT.Relu).then_inc(o_relu, 1)
                act.wait_ge(o_relu, o0 + t + 1)
                act.dma_start(io["h1_dram"][rows_t, 512 * hf:512 * hf + 512], o[u][0:NT, :]).then_inc(o_out[u], 16)
            elif hf == 0:
                act.wait_ge(o_done, o0 + t + 3)
                act.dma_start(io["y_dram"][rows_t, :], o[u][0:NT, :]).then_inc(o_out[u], 16)
            else:
                act.wait_ge(f_var, t + 1)
                act.activation(f_rt[0:NT, :], f_ve[0:NT, :], ACT.Sqrt).then_inc(f_root, 1)
                act.wait_ge(f_norm, t + 1)
                for h, y in enumerate((res[u][0:NT, 1, :], o[u][0:NT, :])):
                    act.activation(rows[u][0:NT, 512 * h:512 * h + 512], y, ACT.Identity, bias=f_sh[u][0:NT, :],
                                   scale=f_rs[u][0:NT, :]).then_inc(f_normed, 1)
                act.wait_ge(f_normed, 2 * t + 6)
                act.dma_start(io["out"][rows_t, :], rows[u][0:NT, :]).then_inc(o_out[u], 16)

        act.wait_ge(bias_in, 32)
        for u in range(2):
            act.sem_inc(o_out[u], 16)
        act.sem_inc(ht_ready, 1)
        act.sem_inc(f_normed, 4)
        for phase in range(len(PHASES)):
            through(act, phase, stage, tile)
        for u in range(2):
            act.wait_ge(o_out[u], 16 * (4 * HF + 1))

    @block.vector
    def _(dve):
        def stage(phase, i, u):
            n0, g0, o0 = counted(phase)
            t = 2 * i + u
            dve.wait_ge(st_hi, n0 + t + 1)
            dve.tensor_tensor(st[u][:, 1, :, :], ht[:, :, bass.ds(t * NT, NT)], raw(st[u][:, 0, :, :]),
                              ALU.subtract).then_inc(st_ready, 1)

        def tile(phase, i, u):
            l, hf, agg = PHASES[phase]
            n0, g0, o0 = counted(phase)
            t = 2 * i + u
            if not agg:
                hi, lo = [g[0:NT, h, bass.ds(t, 1), :].rearrange("p a n -> p (a n)") for h in range(2)]
                dve.wait_ge(g_hi, g0 + t + 1)
                dve.tensor_tensor(lo, ps_g[u][0:NT, :], raw(hi), ALU.subtract).then_inc(g_lo, 1)
                return
            dve.wait_ge(h_used, n0 + t + 3)
            dve.wait_ge(o_out[u], 16 * (HF * (o0 // T) + i) + 16)
            dve.tensor_tensor(o[u][0:NT, :], ps_self[u][0:NT, :], b_rows[0:NT, l, 512 * hf:512 * hf + 512],
                              ALU.add).then_inc(o_biased, 1)
            dve.wait_ge(o_biased, o0 + t + 1)
            if l == 1:
                n = HF * hf + (1 + hf) * i + (1 + hf)
                dve.wait_ge(res_in[u], 16 * n)
                dve.tensor_tensor(o[u][0:NT, :], o[u][0:NT, :], res[u][0:NT, 0, :], ALU.add).then_inc(o_resid, 1)
                dve.wait_ge(o_resid, T * hf + t + 1)
            dve.wait_ge(o_mm, o0 + t + 3)
            dve.scalar_tensor_tensor(out=o[u][0:NT, :], in0=ps_a[u][0:NT, :], scalar=s.deg_inv[0:NT, bass.ds(t, 1)],
                                     in1=o[u][0:NT, :], op0=ALU.mult, op1=ALU.add).then_inc(o_done, 1)
            if l == 1 and hf == 1:
                dve.wait_ge(o_done, o0 + t + 3)
                norm_stats(dve, f_step, 8 * t, f_st[0:NT, :, :], f_mv[0:NT, :], f_ve[0:NT, :], f_var,
                           [res[u][0:NT, 1, :], o[u][0:NT, :]], s.carried)
                dve.wait_ge(f_var, t + 1)
                dve.wait_ge(f_root, t + 1)
                newton_rstd(dve, f_step, 8 * t + 3, f_rs[u][0:NT, :], f_ve[0:NT, :], f_rt[0:NT, :], f_sc[0:NT, :])
                norm_shift(dve, f_sh[u][0:NT, :], f_mv[0:NT, :], f_rs[u][0:NT, :], f_norm)

        dve.sem_inc(g_lo, 2)
        dve.sem_inc(o_done, 2)
        dve.wait_ge(bias_in, 32)
        for phase in range(len(PHASES)):
            through(dve, phase, stage, tile)

    @block.tensor
    def _(pe):
        def turn(l, i, u):
            t = 2 * i + u
            pe.wait_ge(rows_in[u], 16 * (HF * l + i) + 16)
            pe.wait_ge(ht_ready, 2 * (l * T + t) + 1)
            turn_rows(pe, s, u)

        def product(out, u, w):
            for k in range(KD):
                for p, (a, b) in enumerate(HALVES):
                    mm = pe.matmul(out, st[u][:, a, k, :], w[:, b, k * 512:(k + 1) * 512],
                                   start=(k == 0 and p == 0), stop=(k == KD - 1 and p == 2))
            return mm

        def tile(phase, i, u):
            l, hf, agg = PHASES[phase]
            n0, g0, o0 = counted(phase)
            t = 2 * i + u
            pe.wait_ge(st_ready, n0 + t + 1)
            if not agg:
                pe.wait_ge(g_lo, g0 + t + 1)
                product(ps_g[u][0:NT, :], u, s.w_neigh).then_inc(h_used, 1)
                return
            pe.wait_ge(o_done, o0 + t + 1)
            product(ps_self[u][0:NT, :], u, s.w_self).then_inc(h_used, 1)
            pe.wait_ge(g_lo, g0 + 2)
            pe.wait_ge(a_in[u], 16 * (HF * (o0 // T) + i) + 16)

            def products(cast):
                for k in range(T):
                    for h in range(2):
                        mm = pe.matmul(ps_a[u][0:NT, :], cast(a_st[u][0:NT, k, :]), cast(g[0:NT, h, k, :]),
                                       start=(k == 0 and h == 0), stop=(k == T - 1 and h == 1))
                mm.then_inc(o_mm, 1)

            exact_counts(pe, max_degree, products)

        def products(phase):
            first_of_layer, last_of_layer = phase % 4 == 0, phase == 3
            with pe.Fori(0, HF - 1) as i:
                for u in range(2):
                    tile(phase, i, u)
                    if first_of_layer:
                        turn(phase // 4, i + 1, u)
            for u in range(2):
                tile(phase, HF - 1, u)
                if last_of_layer:
                    turn(1, 0, u)

        pe.sem_inc(h_used, 2)
        pe.sem_inc(o_mm, 2)
        max_degree = pe.value_load(s.max_degree[0:1, 0:1], min_val=0, max_val=E)
        turn(0, 0, 1)
        for phase in range(len(PHASES)):
            if phase > 0:
                pe.wait_ge(w_ready, KD * phase)
            products(phase)


class Places:
    pass


def places(nc):
    s = Places()
    at = Map(nc, -(-nc.sbuf_base // 32) * 32)
    s.ident = at("ident", [128, 128], F32)
    s.deg_inv = at("deg_inv", [128, T], F32)
    s.deg = at("deg", [128, T], F32)
    s.max_degree = at("max_degree", [128, 1], I32)
    s.ln_gb = at("ln_gb", [128, 2, KD], F32)
    s.biases = at("biases", [128, 4 + 2 + 3 * 2 * LAYERS + 4], F32)
    s.wide_at = at.at
    s.wide = at("wide", [128, 2, KH, NW], F32R)
    s.at_ = at("a_turned", [128, T, NW], F32R)
    s.work_at = at.at
    at.at += 2 * KD * NW * 4
    s.ring_at = at.at
    s.wring = at("weight_slots", [128, 2, 2, 1024], F32R)
    s.stage_at = at.at
    s.g_at = s.wide_at
    at = Map(nc, s.g_at + 2 * T * 512 * 4)
    s.w_self = at("w_self", [128, 2, KD * 512], F32R)
    s.w_neigh = at("w_neigh", [128, 2, KD * 512], F32R)
    s.rows = [at(f"h_rows{u}", [128, D], F32) for u in range(2)]
    s.sage_bias = at("sage_bias", [128, 2, D], F32)
    s.late_at = at.at
    s.rows_in = [nc.alloc_semaphore(f"rows_in{u}") for u in range(2)]
    s.bias_in = nc.alloc_semaphore("bias_in")
    s.turned = nc.alloc_semaphore("turned")
    s.carried = nc.alloc_semaphore("carried")
    s.banks = [nc.alloc_psum_tensor(f"bank{b}", [128, 512], F32) for b in range(8)]
    return s


def layout(inputs):
    import numpy as np

    a = {name: np.asarray(v) for name, v in inputs.items()}
    g = {name[len("L0_gnn_"):]: v for name, v in a.items() if name.startswith("L0_gnn_")}

    def cols(v):
        return v.reshape(-1, 128).T

    def pair(first, second):
        return np.stack([first, second]).reshape(2, KB, 128, B).transpose(2, 0, 1, 3).reshape(1, 128, 1024)

    empty = np.zeros((B, B), np.float32)
    out = {
        "x": a["x"],
        "src_t": a["src"].reshape(C, EC).T,
        "dst_t": a["dst"].reshape(C, EC).T,
        "pair_weights": np.broadcast_to(np.stack([np.arange(C) // 2 + 1, Q - np.arange(C) // 2])
                                        .astype(np.float32), (EC, 2, C)),
        "iota": np.broadcast_to(np.arange(NW).astype(np.float16), (EC, NW)),
        "ident": np.eye(128, dtype=np.float32),
        "biases": np.concatenate([cols(g["b1"]), cols(g["b2"])] + [cols(g[n]) for n in
                                 ("layer_ba", "layer_ng", "layer_nb")] + [cols(g["bd1"])], 1),
        "bb": g["layer_bb"],
        "W1_pairs": g["W1"].reshape(KD // 2, 2, 128, H).transpose(0, 2, 1, 3).reshape(KD // 2, 128, 2 * H),
        "w_units": np.concatenate([
            g["W2"].reshape(KH, 128, B).transpose(1, 0, 2).reshape(1, 128, 1024),
            pair(g["layer_Wa"][0], empty), pair(g["layer_Wb"][0], g["layer_Wa"][1]),
            g["Wd1"].reshape(KB, 128, H).transpose(1, 0, 2).reshape(1, 128, 1024)]
            + [pair(g["layer_Wb"][i], g["layer_Wa"][i + 1] if i + 1 < LAYERS else empty) for i in range(1, LAYERS)]),
        "Wd2": g["Wd2"],
        "bd2": g["bd2"][None], "out_g": g["out_g"][None], "out_b": g["out_b"][None],
        "w_self": np.stack([a["L1_gnn_W_self0"], a["L1_gnn_W_self1"]]).reshape(2, KD, 128, 2, 512).transpose(0, 3, 1, 2, 4),
        "w_neigh": np.stack([a["L1_gnn_W_neigh0"], a["L1_gnn_W_neigh1"]]).reshape(2, KD, 128, 2, 512).transpose(0, 3, 1, 2, 4),
        "sage_b": np.stack([a["L1_gnn_b0"], a["L1_gnn_b1"]]),
        "ln_gb": np.stack([cols(g["ln_in_g"]), cols(g["ln_in_b"])], 1),
    }
    return {name: np.ascontiguousarray(v) for name, v in out.items()}


def program(nc, io):
    s = places(nc)
    for stage in (graph_block, encoder_block, decoder_block, sage_block):
        with nc.Block() as block:
            stage(nc, block, nc.alloc_semaphore, io, s)


def kernel(**inputs):
    import concourse.bacc as bacc
    import numpy as np
    from concourse.bass_utils import run_bass_kernel_spmd

    nc = bacc.Bacc("TRN2", target_bir_lowering=False, num_devices=1)
    arrays = layout(inputs)
    io = {name: nc.dram_tensor(name, a.shape, mybir.dt.from_np(a.dtype), kind="ExternalInput").ap()
          for name, a in arrays.items()}
    for name, shape in (("at_dram", (T, NT, T, NT)), ("x2_dram", (N, D)), ("h1_dram", (N, D)), ("y_dram", (N, 512))):
        io[name] = nc.dram_tensor(name, shape, F32, kind="Internal").ap()
    io["out"] = nc.dram_tensor("out", (N, D), F32, kind="ExternalOutput").ap()
    program(nc, io)
    r = run_bass_kernel_spmd(nc, [arrays], core_ids=[0])
    return np.asarray(r.results[0]["out"])
```
